# Optimizing a Trainium2 kernel written in Bass

```python
import numpy as np
import jax
import jax.numpy as jnp

def _softmax(x, axis=-1):
    return jax.nn.softmax(x, axis=axis)

def _gelu(x):
    return jax.nn.gelu(x, approximate=True)

def _silu(x):
    return jax.nn.silu(x)

def _sigmoid(x):
    return jax.nn.sigmoid(x)

def _layernorm(x, axis=-1, eps=1e-05):
    m = jnp.mean(x, axis=axis, keepdims=True)
    v = jnp.var(x, axis=axis, keepdims=True)
    return (x - m) / jnp.sqrt(v + eps)

def _scatter_add(tgt, idx, src, axis=0):
    return tgt.at[idx].add(src)

def _segment_sum(src, seg, n):
    return jax.ops.segment_sum(src, seg, n)
kernel_name = 'mk_vit_tower_cls_d1_tok_img1024_r4_167cc9'

def setup_inputs(seed: int=0):
    np.random.seed(seed)
    _w = jnp.asarray

    def _rec_inputs():
        import jax
        import jax.numpy as jnp
        _rk = jax.random.key(seed)
        x = -0.00016672 + 0.999947 * jax.random.normal(jax.random.fold_in(_rk, 1), (32, 3, 96, 96), jnp.float32)
        cls_tok = 0.02 * jax.random.normal(jax.random.fold_in(_rk, 5), (1, 1, 256), jnp.float32)
        return (x, cls_tok)
    x, cls_tok = _rec_inputs()

    def _L0_tok_setup():
        import jax, jax.numpy as jnp
        import numpy as np
        IN_CH, P, EMB, IMG_H, IMG_W = (3, 16, 256, 96, 96)
        N_PATCH = IMG_H // P * (IMG_W // P)
        key = jax.random.key(seed)
        k1, k2, k3, k4, k5 = jax.random.split(key, 5)
        x = jax.random.normal(k1, (64, IN_CH, IMG_H, IMG_W), dtype=jnp.float32)
        W = jax.random.normal(k2, (P * P * IN_CH, EMB), dtype=jnp.float32) * 0.02
        b = jax.random.normal(k3, (EMB,), dtype=jnp.float32) * 0.02
        cls_token = jax.random.normal(k4, (1, 1, EMB), dtype=jnp.float32)
        pos_emb = jax.random.normal(k5, (N_PATCH + 1, EMB), dtype=jnp.float32)
        return {'x': x, 'W': W, 'b': b, 'cls_token': cls_token, 'pos_emb': pos_emb}
    _L0_tok_all = _L0_tok_setup()
    _L0_tok_in = {k: v for k, v in _L0_tok_all.items() if k in ('W', 'b', 'cls_token', 'pos_emb')}
    del _L0_tok_all

    def _L0_attn_setup():
        import jax, jax.numpy as jnp
        import numpy as np
        HIDDEN = 256
        NUM_HEADS = 16
        HEAD_DIM = HIDDEN // NUM_HEADS
        LN_EPS = 1e-05

        def layernorm(x, w, b, eps=LN_EPS):
            mu = jnp.mean(x, axis=-1, keepdims=True)
            var = jnp.mean(jnp.square(x - mu), axis=-1, keepdims=True)
            return (x - mu) * jax.lax.rsqrt(var + eps) * w + b
        key = jax.random.key(seed)
        ks = jax.random.split(key, 7)
        B, S = (4, 512)
        s_in = 1.0 / np.sqrt(HIDDEN)
        return {'hidden_states': jax.random.normal(ks[0], (B, S, HIDDEN), jnp.float32), 'qkv_w': jax.random.uniform(ks[1], (3 * HIDDEN, HIDDEN), jnp.float32, -s_in, s_in), 'qkv_b': jax.random.uniform(ks[2], (3 * HIDDEN,), jnp.float32, -s_in, s_in), 'o_w': jax.random.uniform(ks[3], (HIDDEN, HIDDEN), jnp.float32, -s_in, s_in), 'o_b': jax.random.uniform(ks[4], (HIDDEN,), jnp.float32, -s_in, s_in), 'q_norm_w': jnp.ones((HEAD_DIM,), jnp.float32), 'q_norm_b': jnp.zeros((HEAD_DIM,), jnp.float32), 'k_norm_w': jnp.ones((HEAD_DIM,), jnp.float32), 'k_norm_b': jnp.zeros((HEAD_DIM,), jnp.float32)}
    _L0_attn_all = _L0_attn_setup()
    _L0_attn_in = {k: v for k, v in _L0_attn_all.items() if k in ('qkv_w', 'qkv_b', 'o_w', 'o_b', 'q_norm_w', 'q_norm_b', 'k_norm_w', 'k_norm_b')}
    del _L0_attn_all

    def _L0_ffn_setup():
        import jax, jax.numpy as jnp
        import numpy as np
        DIM = 256
        HIDDEN = 768
        SCALE = 1.0 / 127.0

        def _dequant(w_int, dtype):
            return w_int.astype(dtype) * jnp.asarray(SCALE, dtype)
        key = jax.random.key(seed)
        k_x, k_g, k_u, k_d = jax.random.split(key, 4)
        x = jax.random.normal(k_x, (4, 512, DIM), dtype=jnp.float32)
        w_gate = jax.random.randint(k_g, (HIDDEN, DIM), -127, 128, dtype=jnp.int32)
        w_up = jax.random.randint(k_u, (HIDDEN, DIM), -127, 128, dtype=jnp.int32)
        w_down = jax.random.randint(k_d, (DIM, HIDDEN), -127, 128, dtype=jnp.int32)
        return {'x': x, 'w_gate': w_gate, 'w_up': w_up, 'w_down': w_down}
    _L0_ffn_all = _L0_ffn_setup()
    _L0_ffn_in = {k: v for k, v in _L0_ffn_all.items() if k in ('w_gate', 'w_up', 'w_down')}
    del _L0_ffn_all
    return {'x': x, 'cls_tok': cls_tok, 'L0_tok_W': _L0_tok_in['W'], 'L0_tok_b': _L0_tok_in['b'], 'L0_tok_cls_token': _L0_tok_in['cls_token'], 'L0_tok_pos_emb': _L0_tok_in['pos_emb'], 'L0_attn_qkv_w': _L0_attn_in['qkv_w'], 'L0_attn_qkv_b': _L0_attn_in['qkv_b'], 'L0_attn_o_w': _L0_attn_in['o_w'], 'L0_attn_o_b': _L0_attn_in['o_b'], 'L0_attn_q_norm_w': _L0_attn_in['q_norm_w'], 'L0_attn_q_norm_b': _L0_attn_in['q_norm_b'], 'L0_attn_k_norm_w': _L0_attn_in['k_norm_w'], 'L0_attn_k_norm_b': _L0_attn_in['k_norm_b'], 'L0_ffn_w_gate': _L0_ffn_in['w_gate'], 'L0_ffn_w_up': _L0_ffn_in['w_up'], 'L0_ffn_w_down': _L0_ffn_in['w_down']}

def reference(x, cls_tok, L0_tok_W, L0_tok_b, L0_tok_cls_token, L0_tok_pos_emb, L0_attn_qkv_w, L0_attn_qkv_b, L0_attn_o_w, L0_attn_o_b, L0_attn_q_norm_w, L0_attn_q_norm_b, L0_attn_k_norm_w, L0_attn_k_norm_b, L0_ffn_w_gate, L0_ffn_w_up, L0_ffn_w_down):
    import jax
    import jax.numpy as jnp

    def _L0_tok_ref(x, W, b, cls_token, pos_emb):
        import jax, jax.numpy as jnp
        import numpy as np
        IN_CH, P, EMB, IMG_H, IMG_W = (3, 16, 256, 96, 96)
        N_PATCH = IMG_H // P * (IMG_W // P)
        B, C, H, Wd = x.shape
        p = P
        xp = x.reshape(B, C, H // p, p, Wd // p, p)
        xp = jnp.transpose(xp, (0, 2, 4, 3, 5, 1)).reshape(B, -1, p * p * C)
        tok = jnp.einsum('bnf,fe->bne', xp, W) + b
        cls = jnp.broadcast_to(cls_token, (B, 1, tok.shape[-1]))
        out = jnp.concatenate([cls, tok], axis=1) + pos_emb
        return out

    def _L0_attn_ref(hidden_states, qkv_w, qkv_b, o_w, o_b, q_norm_w, q_norm_b, k_norm_w, k_norm_b):
        import jax, jax.numpy as jnp
        import numpy as np
        HIDDEN = 256
        NUM_HEADS = 16
        HEAD_DIM = HIDDEN // NUM_HEADS
        LN_EPS = 1e-05

        def layernorm(x, w, b, eps=LN_EPS):
            mu = jnp.mean(x, axis=-1, keepdims=True)
            var = jnp.mean(jnp.square(x - mu), axis=-1, keepdims=True)
            return (x - mu) * jax.lax.rsqrt(var + eps) * w + b
        B, S, _ = hidden_states.shape
        H, D = (NUM_HEADS, HEAD_DIM)
        qkv = hidden_states @ qkv_w.T + qkv_b
        q, k, v = jnp.split(qkv, 3, axis=-1)
        q = q.reshape(B, S, H, D)
        k = k.reshape(B, S, H, D)
        v = v.reshape(B, S, H, D)
        q = layernorm(q, q_norm_w, q_norm_b)
        k = layernorm(k, k_norm_w, k_norm_b)
        scale = 1.0 / np.sqrt(D).astype(np.float32)
        scores = jnp.einsum('bqhd,bkhd->bhqk', q, k) * scale
        weights = jax.nn.softmax(scores, axis=-1)
        attn = jnp.einsum('bhqk,bkhd->bqhd', weights, v)
        attn = attn.reshape(B, S, H * D)
        return attn @ o_w.T + o_b

    def _L0_ffn_ref(x, w_gate, w_up, w_down):
        import jax, jax.numpy as jnp
        import numpy as np
        DIM = 256
        HIDDEN = 768
        SCALE = 1.0 / 127.0

        def _dequant(w_int, dtype):
            return w_int.astype(dtype) * jnp.asarray(SCALE, dtype)
        wg = _dequant(w_gate, x.dtype)
        wu = _dequant(w_up, x.dtype)
        wd = _dequant(w_down, x.dtype)
        gate = jnp.einsum('bsd,hd->bsh', x, wg)
        up = jnp.einsum('bsd,hd->bsh', x, wu)
        h = jax.nn.silu(gate) * up
        return jnp.einsum('bsh,dh->bsd', h, wd)
    h = _L0_tok_ref(x, L0_tok_W, L0_tok_b, L0_tok_cls_token, L0_tok_pos_emb)
    h = jnp.concatenate([jnp.broadcast_to(cls_tok, (h.shape[0], 1, h.shape[2])), h], axis=1)
    h = h + _L0_attn_ref(_layernorm(h, axis=-1), L0_attn_qkv_w, L0_attn_qkv_b, L0_attn_o_w, L0_attn_o_b, L0_attn_q_norm_w, L0_attn_q_norm_b, L0_attn_k_norm_w, L0_attn_k_norm_b)
    h = h + _L0_ffn_ref(_layernorm(h, axis=-1), L0_ffn_w_gate, L0_ffn_w_up, L0_ffn_w_down)
    return h

_drawn_inputs = setup_inputs


def setup_inputs(seed=0):
    import zlib

    import numpy as np

    out = dict(_drawn_inputs(seed))
    spreads = {'L0_attn_q_norm_w': (1.0, 0.2),
     'L0_attn_q_norm_b': (0.0, 0.45),
     'L0_attn_k_norm_w': (1.0, 0.6),
     'L0_attn_k_norm_b': (0.0, 0.8)}
    factors = {}
    for name, (base, spread) in spreads.items():
        noise = np.random.default_rng([zlib.crc32(name.encode()), seed]).standard_normal(out[name].shape)
        drawn = base * np.exp(spread * noise) if base else spread * noise
        out[name] = jnp.asarray(drawn.astype(out[name].dtype))
    for name, factor in factors.items():
        out[name] = (out[name] * factor).astype(out[name].dtype)
    return out
```

```python
from contextlib import ExitStack

import concourse.bass as bass
from concourse import mybir
from concourse.alu_op_type import AluOpType as ALU

ACT = mybir.ActivationFunctionType
F32 = mybir.dt.float32
F16 = mybir.dt.float16
I32 = mybir.dt.int32
AX = mybir.AxisListType

P = 128
BANK = 512

IMAGES, CH, SIDE, PATCH = 32, 3, 96, 16
GRID = SIDE // PATCH
EMB = 256
KE = EMB // P
TOK = GRID * GRID + 2
FEAT = CH * PATCH * PATCH
KF = FEAT // P
HALF = PATCH // 2

GI = 3
GT = GI * TOK
NG = -(-IMAGES // GI)
LAST_ROWS = (IMAGES - GI * (NG - 1)) * TOK
XIMG = 16
XROWS = XIMG * GRID
XTILES = IMAGES // XIMG

HEADS, HD = 16, 16
QKV = 3 * EMB
HG = 4
PAIR = 2 * TOK
HID = 768
MT = HID // P
CG = 3
NCH = NG // CG
LN_EPS = 1e-5
QUANT = 1.0 / 127.0
XSCALE = 2.0 ** 11
HSCALE = 2.0 ** -3


class Group:

    def __init__(self, i, c):
        self.n = 2 * i + c
        self.buf = c % 2
        self.turn = i + c // 2
        self.real = not isinstance(self.n, int) or 0 <= self.n < NG


def positive(n):
    return not isinstance(n, int) or n > 0


def vit_kernel(nc, x, cls_tok, w_emb, b_emb, cls_token, pos_emb, qkv_w, qkv_b, o_w, o_b,
               qn_w, qn_b, kn_w, kn_b, w_gate, w_up, w_down, out):
    with ExitStack() as ctx:
        def sb(name, shape, dt=F32):
            return ctx.enter_context(nc.sbuf_tensor(name, shape, dt))

        def sem(name):
            return ctx.enter_context(nc.semaphore(name))

        ident = sb("ident", [P, P])
        ident16 = sb("ident16", [P, P], F16)
        xrow = sb("xrow", [P, XTILES, CH, PATCH, GRID, PATCH])
        xcut = sb("xcut", [P, CH, 2, GRID, HALF * PATCH])
        xpt = sb("xpt", [P, KF, NG * GI, TOK])
        xs = sb("xs", [P, 2, KF, GT])
        wemb = sb("wemb", [P, CH, 2, EMB])
        wqkv_raw = sb("wqkv_raw", [P, QKV // P, EMB])
        wqkv = sb("wqkv", [P, KE, QKV])
        wo_raw = sb("wo_raw", [P, KE, EMB])
        wo = sb("wo", [P, KE, EMB])
        wmean = sb("wmean", [P, KE, 2 * HEADS])
        bqkv = sb("bqkv", [P, QKV])
        bmean = sb("bmean", [P, 2 * HEADS])
        bo = sb("bo", [P, EMB])
        tok_pos = sb("tok_pos", [P, EMB])
        tok_add = sb("tok_add", [P, EMB])
        lnp = sb("lnp", [P, 4])
        par = sb("par", [P, 2])
        klnw = sb("klnw", [P, 2])
        klnb = sb("klnb", [P, 2])
        mhalf = sb("mhalf", [P, 2 * HEADS])

        h_emb = sb("h_emb", [P, 2, EMB])
        stats1 = sb("stats1", [P, 2, 6])
        mv1 = sb("mv1", [P, 2, 2])
        ve1 = sb("ve1", [P, 2])
        rstd1 = sb("rstd1", [P, 2])
        xn1 = sb("xn1", [P, 2, EMB])
        x1t = sb("x1t", [P, 2, KE, GT])
        qk = sb("qk", [P, 2, 2 * EMB])
        sq = sb("sq", [P, 2 * EMB])
        ss = sb("ss", [P, 2, 2 * HEADS])
        ve_qk = sb("ve_qk", [P, 2 * HEADS])
        rstd_qk = sb("rstd_qk", [P, 2 * HEADS])
        vt = sb("vt", [P, 2, 2, HD, HEADS // 2])
        v2 = sb("v2", [PAIR, 2, GI, 2 * HD, HEADS // 2])
        qm = sb("qm", [P, KE, GI * (GT + TOK)])
        k2 = sb("k2", [P, KE, 2, GT])
        prob = sb("prob", [P, 2, HG, 2 * 2, TOK])
        smax = sb("smax", [P, 2, HEADS])
        ssum = sb("ssum", [P, 2, HEADS])
        rsum = sb("rsum", [P, 2, HEADS])
        pt = sb("pt", [PAIR, HG * 2, GT])
        ot = sb("ot", [P, KE, GT])
        h2 = sb("h2", [P, NG, EMB])
        hcur = sb("hcur", [P, EMB])
        stats2 = sb("stats2", [P, 6])
        mv2 = sb("mv2", [P, 2])
        ve2 = sb("ve2", [P, 1])
        rstd2 = sb("rstd2", [P, 1])
        xn2 = sb("xn2", [P, EMB])
        x2hi = sb("x2hi", [P, KE, NG * GT], F16)
        x2lo = sb("x2lo", [P, KE, NG * GT], F16)

        wraw = xrow.rearrange("p t c a w b -> p t (c a w b)")[:, 0].bitcast(I32).rearrange("p (n e) -> p n e", n=3)
        w16 = sb("w16", [P, 3, MT * EMB], F16)
        wgt = sb("wgt", [P, KE, HID], F16)
        wut = sb("wut", [P, KE, HID], F16)
        wdt = sb("wdt", [P, MT, EMB], F16)
        sil = sb("sil", [P, 2, CG * GT])
        hf = sb("hf", [P, 2, CG * GT])
        hhi = sb("hhi", [P, 2, CG * GT], F16)
        hlo = sb("hlo", [P, 2, CG * GT], F16)

        ps = [ctx.enter_context(nc.psum_tensor(f"ps{b}", [P, BANK], F32)) for b in range(4, 8)]
        score_ps = ctx.enter_context(nc.psum_tensor("score_ps", [P, HG, BANK], F32))
        ptq_ps0, ptq_ps1, out_ps, emb_ps = ps

        x_loaded = [sem(f"x_loaded{t}") for t in range(XTILES)]
        wemb_loaded, wqkv_loaded, wo_loaded = sem("wemb_loaded"), sem("wqkv_loaded"), sem("wo_loaded")
        ffn_loaded = [sem(f"ffn_loaded{i}") for i in range(3)]
        rows_loaded, cols_loaded = sem("rows_loaded"), sem("cols_loaded")
        ident_zero, ident_ready, ident16_ready = sem("ident_zero"), sem("ident_ready"), sem("ident16_ready")
        rows_zeroed, xpt_zeroed, qm_zeroed = sem("rows_zeroed"), sem("xpt_zeroed"), sem("qm_zeroed")
        consts_ready, par_ready, tok_added, qkv_w_centred = sem("consts_ready"), sem("par_ready"), sem("tok_added"), sem("qkv_w_centred")
        means_done, bmeans_done, kln_ready = sem("means_done"), sem("bmeans_done"), sem("kln_ready")
        xcut_ready = sem("xcut_ready")
        xt_done, xt_evac_act, xt_evac_dve = sem("xt_done"), sem("xt_evac_act"), sem("xt_evac_dve")
        wt_done, wt_evac = sem("wt_done"), sem("wt_evac")

        xs_loaded = [sem(f"xs_loaded{b}") for b in range(2)]
        v_moved = [sem(f"v_moved{b}") for b in range(2)]
        emb_done, x1t_done, qkv_done = sem("emb_done"), sem("x1t_done"), sem("qkv_done")
        qkt_done, scores_done, pt_done = sem("qkt_done"), sem("scores_done"), sem("pt_done")
        v2_free, o_done, x2t_done = sem("v2_free"), sem("o_done"), sem("x2t_done")
        h_ready, stats1_done, mv1_done, ve1_done = sem("h_ready"), sem("stats1_done"), sem("mv1_done"), sem("ve1_done")
        rstd1_done, xn1_done = sem("rstd1_done"), sem("xn1_done")
        res_ready, x1t_evac = sem("res_ready"), sem("x1t_evac")
        qk_ready, v_ready, sq_done, ss_done = sem("qk_ready"), sem("v_ready"), sem("sq_done"), sem("ss_done")
        ve_qk_done, rstd_qk_done, qkn_done, qkt_evac = sem("ve_qk_done"), sem("rstd_qk_done"), sem("qkn_done"), sem("qkt_evac")
        max_done, sub_done, exp_done, sum_done = sem("max_done"), sem("sub_done"), sem("exp_done"), sem("sum_done")
        rsum_done, probs_ready, pt_evac, ot_evac = sem("rsum_done"), sem("probs_ready"), sem("pt_evac"), sem("ot_evac")
        h2_kept = sem("h2_kept")
        h2_ready, stats2_done, mv2_done, ve2_done = sem("h2_ready"), sem("stats2_done"), sem("mv2_done"), sem("ve2_done")
        rstd2_done, xn2_done, x2hi_done, x2lo_done = sem("rstd2_done"), sem("xn2_done"), sem("x2hi_done"), sem("x2lo_done")

        w16_ready, fwt_done, fwt_evac = sem("w16_ready"), sem("fwt_done"), sem("fwt_evac")
        gu_done, silu_done, hf_done = sem("gu_done"), sem("silu_done"), sem("hf_done")
        hhi_done, hlo_done, down_done = sem("hhi_done"), sem("hlo_done"), sem("down_done")
        y_ready, y_stored = sem("y_ready"), sem("y_stored")

        out_rows = out.rearrange("b t e -> (b t) e")
        FW_SETS = MT * KE
        FW_BATCH = 4
        XT_WP = 3
        XT_BATCHES = KF * (GRID // XT_WP)
        W_BATCHES = (QKV // P) * KE // 4 + KE * KE // 4

        steady = (NG - 2 - 1) // 2

        def slots(eng, run_slot):
            for s in range(-2, 1):
                run_slot(0, s)
            with eng.Fori(0, steady) as i:
                run_slot(i, 1)
                run_slot(i, 2)
            for s in range(1 + 2 * steady, NG + 1):
                run_slot(0, s)

        block = ctx.enter_context(nc.Block())

        @block.sync
        def _(sp):
            x_dram = x.rearrange("b c (hp p1) w -> b hp c (p1 w)", p1=PATCH)
            xrow_flat = xrow.rearrange("p t c a w b -> p t c (a w b)")

            def load_x(t):
                for c in range(CH):
                    sp.dma_start(xrow_flat[0:XROWS, t, c], x_dram[t * XIMG:(t + 1) * XIMG, :, c]).then_inc(x_loaded[t], 16)

            load_x(0)
            sp.dma_start(wqkv_raw[:], qkv_w.rearrange("(t p) k -> p t k", p=P)).then_inc(wqkv_loaded, 16)
            sp.dma_start(wo_raw[:], o_w.rearrange("(t p) k -> p t k", p=P)).then_inc(wo_loaded, 16)
            w_dram = w_emb.rearrange("(h p c) e -> p h (c e)", h=2, p=P)
            for hh in range(2):
                sp.dma_start(wemb[:, :, hh, :], w_dram[:, hh].rearrange("p (c e) -> p c e", c=CH)).then_inc(wemb_loaded, 16)
            for n, v in enumerate((qn_w, qn_b, kn_w, kn_b)):
                sp.dma_start(lnp[:, n:n + 1], v.partition_broadcast(P // HD).rearrange("r (d a) -> r d a", a=1)).then_inc(cols_loaded, 16)
            load_x(1)
            sp.wait_ge(xcut_ready, KF)
            for n, w in enumerate((w_gate, w_up)):
                sp.dma_start(wraw[:, n].rearrange("p (t k) -> p t k", t=MT), w.rearrange("(t p) k -> p t k", p=P)).then_inc(ffn_loaded[n], 16)
            sp.dma_start(wraw[:, 2].rearrange("p (t k) -> p t k", t=KE), w_down.rearrange("(t p) k -> p t k", p=P)).then_inc(ffn_loaded[2], 16)

            def move_v(g):
                if not g.real:
                    return
                count = g.n + 1
                sp.wait_ge(v_ready, count)
                sp.wait_ge(v2_free, count)
                for im in range(GI):
                    for hp in range(2):
                        sp.dma_start(v2[hp * TOK:(hp + 1) * TOK, g.buf, im, hp * HD:(hp + 1) * HD], vt[im * TOK:(im + 1) * TOK, g.buf, hp]).then_inc(v_moved[g.buf], 16)


            def slot(i, s):
                move_v(Group(i, s + 1))

            slots(sp, slot)

            for g in range(NG):
                sp.wait_ge(y_ready, g + 1)
                rows = GT if g < NG - 1 else LAST_ROWS
                sp.dma_start(out_rows[g * GT:g * GT + rows], h2[0:rows, g]).then_inc(y_stored, 16)
            sp.wait_ge(y_stored, 16 * NG)

        @block.gpsimd
        def _(pool):
            nc.gpsimd.memset(ident[:], 0.0).then_inc(ident_zero, 1)
            pool.wait_ge(ident_zero, 1)
            nc.gpsimd.affine_select(out=ident[:], in_=ident[:], compare_op=ALU.not_equal, fill=1.0, base=0,
                                    pattern=[[-1, P]], channel_multiplier=1).then_inc(ident_ready, 1)
            nc.gpsimd.memset(tok_pos[:], 0.0).then_inc(rows_zeroed, 1)
            nc.gpsimd.memset(xpt.rearrange("p k b t -> p k b t")[:, :, IMAGES:NG * GI, :], 0.0)
            nc.gpsimd.memset(xpt[:, :, 0:IMAGES, 0:2], 0.0).then_inc(xpt_zeroed, 1)
            nc.gpsimd.memset(mhalf[:], -0.5).then_inc(consts_ready, 1)
            nc.gpsimd.memset(qm[:], 0.0).then_inc(qm_zeroed, 1)
            for b in range(2):
                nc.gpsimd.memset(v2[:, b], 0.0).then_inc(v2_free, 1)

            pool.wait_ge(rows_zeroed, 1)
            for im in range(GI):
                r = im * TOK
                pool.dma_start(tok_pos[r + 1:r + TOK], pos_emb).then_inc(rows_loaded, 16)
                pool.dma_start(tok_add[r:r + 1], cls_tok.rearrange("a b e -> (a b) e")).then_inc(rows_loaded, 16)
                pool.dma_start(tok_add[r + 1:r + 2], cls_token.rearrange("a b e -> (a b) e")).then_inc(rows_loaded, 16)
                pool.dma_start(tok_add[r + 2:r + TOK], b_emb.partition_broadcast(TOK - 2)).then_inc(rows_loaded, 16)
            pool.dma_start(bqkv[0:GT], qkv_b.partition_broadcast(GT)).then_inc(rows_loaded, 16)
            pool.dma_start(bo[0:GT], o_b.partition_broadcast(GT)).then_inc(rows_loaded, 16)

            def residual(g):
                if not g.real:
                    return
                pool.wait_ge(h_ready, g.n + 1)
                nc.gpsimd.tensor_tensor(h2[0:GT, g.n], h_emb[0:GT, g.buf], bo[0:GT], ALU.add).then_inc(res_ready, 1)

            def rstd_of_tokens(g):
                if not g.real:
                    return
                pool.wait_ge(ve1_done, g.n + 1)
                nc.gpsimd.tensor_tensor(rstd1[0:GT, g.buf:g.buf + 1], ve1[0:GT, g.buf:g.buf + 1],
                                        mhalf[0:GT, 0:1], ALU.pow).then_inc(rstd1_done, 1)

            def rstd_of_residual(g):
                if not g.real:
                    return
                pool.wait_ge(ve2_done, g.n + 1)
                nc.gpsimd.tensor_tensor(rstd2[0:GT], ve2[0:GT], mhalf[0:GT, 0:1], ALU.pow).then_inc(rstd2_done, 1)

            def keep_residual(g):
                if not g.real:
                    return
                pool.wait_ge(h2_ready, g.n + 1)
                nc.gpsimd.tensor_copy(h2[0:GT, g.n], hcur[0:GT]).then_inc(h2_kept, 1)

            def norm_qk(g):
                if not g.real:
                    return
                pool.wait_ge(ve_qk_done, g.n + 1)
                nc.gpsimd.tensor_tensor(rstd_qk[0:GT], ve_qk[0:GT], mhalf[0:GT], ALU.pow).then_inc(rstd_qk_done, 1)
                pool.wait_ge(rstd_qk_done, g.n + 1)
                view = qk[0:GT, g.buf].rearrange("p (h d) -> p h d", d=HD)
                nc.gpsimd.tensor_tensor(view, view, rstd_qk[0:GT].unsqueeze(2).to_broadcast([GT, 2 * HEADS, HD]),
                                        ALU.mult).then_inc(qkn_done, 1)

            def norm_probs(g):
                if not g.real:
                    return
                pool.wait_ge(rsum_done, g.n + 1)
                view = prob[0:GT, g.buf].rearrange("p j h k -> p (j h) k")
                nc.gpsimd.tensor_tensor(view, view, rsum[0:GT, g.buf].unsqueeze(2).to_broadcast([GT, HEADS, TOK]),
                                        ALU.mult).then_inc(probs_ready, 1)

            pool.wait_ge(rows_loaded, 16 * (4 * GI + 2))

            def slot(i, s):
                rstd_of_tokens(Group(i, s + 2))
                norm_probs(Group(i, s))
                residual(Group(i, s + 2))
                rstd_of_residual(Group(i, s - 1))
                keep_residual(Group(i, s - 1))
                norm_qk(Group(i, s + 2))

            slots(pool, slot)

        @block.tensor
        def _(pe):
            pe.wait_ge(ident_ready, 1)
            n = 0
            for t in range(XTILES):
                for f in range(KF):
                    pe.wait_ge(xcut_ready, t * KF + f + 1)
                    for w0 in range(0, GRID, XT_WP):
                        bank = score_ps[:, n % HG]
                        if n >= HG:
                            pe.wait_ge(xt_evac_act if n % 2 == 0 else xt_evac_dve, (n - HG) // 2 + 1)
                        for w in range(XT_WP):
                            src = xcut[0:XROWS, f // 2, f % 2, w0 + w]
                            mm = pe.transpose(bank[:, w * XROWS:(w + 1) * XROWS], src, ident[0:XROWS, 0:XROWS])
                        mm.then_inc(xt_done, 1)
                        n += 1
                if t == 0:
                    pe.wait_ge(wqkv_loaded, 16)
                    pe.wait_ge(wo_loaded, 16)
                    m = 0
                    for raw, tiles in ((wqkv_raw, QKV // P), (wo_raw, KE)):
                        for k in range(KE):
                            for r0 in range(0, tiles, 3 if tiles > KE else 2):
                                step = 3 if tiles > KE else 2
                                if m >= 2:
                                    pe.wait_ge(wt_evac, m - 1)
                                for r in range(step):
                                    mm = pe.transpose(ps[m % 2][:, r * P:(r + 1) * P], raw[:, r0 + r, k * P:(k + 1) * P], ident[:])
                                mm.then_inc(wt_done, 1)
                                m += 1
            pe.wait_ge(wemb_loaded, 32)
            pe.wait_ge(qkv_w_centred, 3)
            pe.wait_ge(wt_evac, 6)

            def embed(g):
                if not g.real:
                    return
                pe.wait_ge(xs_loaded[g.buf], 16 * (g.turn + 1))
                if positive(g.n - 1):
                    pe.wait_ge(qkt_evac, 3 * (g.n - 1))
                for f in range(KF):
                    mm = pe.matmul(emb_ps[0:GT, 0:EMB], xs[:, g.buf, f], wemb[:, f // 2, f % 2], start=(f == 0), stop=(f == KF - 1))
                mm.then_inc(emb_done, 1)

            def turn_xn1(g):
                if not g.real:
                    return
                pe.wait_ge(xn1_done, g.n + 1)
                for k in range(KE):
                    mm = pe.transpose(emb_ps[:, k * GT:(k + 1) * GT], xn1[0:GT, g.buf, k * P:(k + 1) * P], ident[0:GT, 0:GT])
                mm.then_inc(x1t_done, 1)

            def project_qkv(g):
                if not g.real:
                    return
                pe.wait_ge(x1t_evac, g.n + 1)
                if positive(g.n - 2):
                    pe.wait_ge(pt_evac, 2 * (g.n - 2))
                for k in range(KE):
                    pe.matmul(ptq_ps0[0:GT], x1t[:, g.buf, k], wqkv[:, k, 0:2 * EMB], start=(k == 0), stop=(k == KE - 1))
                for k in range(KE):
                    mm = pe.matmul(ptq_ps1[0:GT, 0:EMB], x1t[:, g.buf, k], wqkv[:, k, 2 * EMB:QKV], start=(k == 0), stop=(k == KE - 1))
                mm.then_inc(qkv_done, 1)

            def turn_qk(g):
                if not g.real:
                    return
                pe.wait_ge(qkn_done, g.n + 1)
                if g.real and (not isinstance(g.n, int) or g.n + 1 < NG):
                    pe.wait_ge(x1t_evac, g.n + 2)
                for k in range(2 * KE):
                    mm = pe.transpose(emb_ps[:, k * GT:(k + 1) * GT], qk[0:GT, g.buf, k * P:(k + 1) * P], ident[0:GT, 0:GT])
                mm.then_inc(qkt_done, 1)

            def scores(g):
                if not g.real:
                    return
                pe.wait_ge(qkt_evac, 3 * (g.n + 1))
                if positive(g.n):
                    pe.wait_ge(sub_done, g.n)
                for a in range(KE):
                    for im in range(GI):
                        for j in range(HG):
                            rows = slice(j * 32, (j + 1) * 32)
                            mm = pe.matmul(score_ps[0:GT, j, a * PAIR:(a + 1) * PAIR],
                                           qm[rows, a, im * GT:(im + 1) * GT],
                                           k2[rows, a, :, im * TOK:(im + 1) * TOK],
                                           start=(im == 0), stop=(im == GI - 1))
                mm.then_inc(scores_done, 1)

            def turn_probs(g):
                if not g.real:
                    return
                pe.wait_ge(probs_ready, g.n + 1)
                if not isinstance(g.n, int) or g.n + 2 < NG:
                    pe.wait_ge(qk_ready, g.n + 3)
                    pe.wait_ge(v_ready, g.n + 3)
                for c in range(2 * HG):
                    bank = ptq_ps0 if c < HG else ptq_ps1
                    src = prob[0:GT, g.buf].rearrange("p j h k -> p (j h k)")[:, c * PAIR:(c + 1) * PAIR]
                    mm = pe.transpose(bank[0:PAIR, (c % HG) * GT:(c % HG + 1) * GT], src, ident[0:GT, 0:GT])
                    if c % HG == HG - 1:
                        mm.then_inc(pt_done, 1)

            def attend(g):
                if not g.real:
                    return
                pe.wait_ge(pt_evac, 2 * (g.n + 1))
                pe.wait_ge(v_moved[g.buf], 16 * 2 * GI * (g.turn + 1))
                if positive(g.n):
                    pe.wait_ge(x2lo_done, g.n)
                for a in range(KE):
                    for im in range(GI):
                        for j in range(HG):
                            mm = pe.matmul(out_ps[j * 32:(j + 1) * 32, a * GT + im * TOK:a * GT + (im + 1) * TOK],
                                           v2[:, g.buf, im, :, a * HG + j],
                                           pt[:, 2 * j + a, im * TOK:(im + 1) * TOK], start=True, stop=True)
                mm.then_inc(v2_free, 1)

            def project_out(g):
                if not g.real:
                    return
                pe.wait_ge(ot_evac, g.n + 1)
                for k in range(KE):
                    mm = pe.matmul(out_ps[0:GT, 0:EMB], ot[:, k], wo[:, k], start=(k == 0), stop=(k == KE - 1))
                mm.then_inc(o_done, 1)

            def turn_xn2(g):
                if not g.real:
                    return
                pe.wait_ge(xn2_done, g.n + 1)
                for k in range(KE):
                    mm = pe.transpose(out_ps[:, k * GT:(k + 1) * GT], xn2[0:GT, k * P:(k + 1) * P], ident[0:GT, 0:GT])
                mm.then_inc(x2t_done, 1)

            def slot(i, s):
                scores(Group(i, s))
                turn_probs(Group(i, s - 1))
                embed(Group(i, s + 2))
                attend(Group(i, s - 1))
                turn_xn1(Group(i, s + 2))
                project_out(Group(i, s - 1))
                turn_qk(Group(i, s + 1))
                project_qkv(Group(i, s + 2))
                turn_xn2(Group(i, s - 1))

            slots(pe, slot)

            pe.wait_ge(ident16_ready, 1)
            pe.wait_ge(w16_ready, 3)
            for b in range(3 * FW_SETS // FW_BATCH):
                if b == 0:
                    pe.wait_ge(sub_done, NG)
                if b >= 2:
                    pe.wait_ge(fwt_evac, b - 1)
                bank = score_ps[:, b % 2].bitcast(F16)
                for q in range(FW_BATCH):
                    n = b * FW_BATCH + q
                    w, n = n // FW_SETS, n % FW_SETS
                    src = w16[:, w, n * P:(n + 1) * P]
                    mm = pe.transpose(bank[:, q * P:(q + 1) * P], src, ident16[:])
                mm.then_inc(fwt_done, 1)
            pe.wait_ge(fwt_evac, 3 * FW_SETS // FW_BATCH)
            pe.wait_ge(x2lo_done, NG)
            pe.wait_ge(pt_evac, 2 * NG)

            acc = (ptq_ps0, ptq_ps1, out_ps)

            def gate_up(c, m, groups):
                T = groups * GT
                n = c * MT + m
                if positive(n - 1):
                    pe.wait_ge(hf_done, n - 1)
                for b, w in ((m % 2, wgt), (2 + m % 2, wut)):
                    step = 0
                    for k in range(KE):
                        for part in (x2hi, x2lo):
                            mm = pe.matmul(score_ps[:, b, 0:T], w[:, k, m * P:(m + 1) * P], part[:, k, bass.ds(c * (CG * GT), T)],
                                           start=(step == 0), stop=(step == 2 * KE - 1))
                            step += 1
                mm.then_inc(gu_done, 1)

            def down(c, m, groups):
                pe.wait_ge(hhi_done, c * MT + m + 1)
                pe.wait_ge(hlo_done, c * MT + m + 1)
                if m == 0 and positive(c):
                    pe.wait_ge(y_ready, c * CG)
                for q in range(groups):
                    for part in (hhi, hlo):
                        mm = pe.matmul(acc[q][0:GT, 0:EMB], part[:, m % 2, q * GT:(q + 1) * GT], wdt[:, m],
                                       start=(m == 0 and part is hhi), stop=(m == MT - 1 and part is hlo))
                mm.then_inc(down_done, 1)

            def chunk(c, groups):
                for m in range(MT):
                    gate_up(c, m, groups)
                    if m >= 1:
                        down(c, m - 1, groups)
                down(c, MT - 1, groups)

            chunk(0, CG)
            with pe.Fori(1, NCH) as c:
                chunk(c, CG)
            chunk(NCH, NG - NCH * CG)

        @block.scalar
        def _(act):
            n = 0
            for t in range(XTILES):
                for f in range(KF):
                    for w0 in range(0, GRID, XT_WP):
                        if n % 2 == 0:
                            act.wait_ge(xt_done, n + 1)
                            nc.scalar.copy(
                                xpt[:, f, t * XIMG:(t + 1) * XIMG, 2:TOK].rearrange("p b (hp wp) -> p wp b hp", wp=GRID)[:, w0:w0 + XT_WP],
                                score_ps[:, n % HG, 0:XT_WP * XROWS].rearrange("p (wp b hp) -> p wp b hp", wp=XT_WP, b=XIMG),
                            ).then_inc(xt_evac_act, 1)
                        n += 1
                if t == 0:
                    for m in range(4):
                        act.wait_ge(wt_done, m + 1)
                        nc.scalar.copy(wqkv[:, m // 2, (m % 2) * 3 * P:(m % 2 + 1) * 3 * P], ps[m % 2][:, 0:3 * P]).then_inc(wt_evac, 1)
                    for m in range(4, 6):
                        act.wait_ge(wt_done, m + 1)
                        nc.scalar.copy(wo[:, m - 4], ps[m % 2][:, 0:EMB]).then_inc(wt_evac, 1)
            act.wait_ge(xt_evac_act, XTILES * XT_BATCHES // 2)
            act.wait_ge(xt_evac_dve, XTILES * XT_BATCHES // 2)
            act.wait_ge(xpt_zeroed, 1)
            act.wait_ge(kln_ready, 1)
            act.wait_ge(qm_zeroed, 1)

            def load_xs(g):
                if not g.real:
                    return
                if positive(g.n - 1):
                    act.wait_ge(emb_done, g.n - 1)
                act.dma_start(xs[:, g.buf], xpt.rearrange("p k b t -> p k (b t)")[:, :, bass.ds(g.n * GT, GT)]).then_inc(xs_loaded[g.buf], 16)

            def evac_pt(g):
                if not g.real:
                    return
                if positive(g.n):
                    act.wait_ge(v2_free, g.n + 2)
                for b in range(2):
                    act.wait_ge(pt_done, 2 * g.n + b + 1)
                    nc.scalar.copy(pt[:, b * HG:(b + 1) * HG], (ptq_ps0, ptq_ps1)[b][0:PAIR, 0:HG * GT].rearrange("p (c t) -> p c t", c=HG)).then_inc(pt_evac, 1)

            def exponentials(g):
                if not g.real:
                    return
                act.wait_ge(sub_done, g.n + 1)
                view = prob[0:GT, g.buf].rearrange("p j h k -> p (j h k)")
                nc.scalar.activation(view, view, ACT.Exp, scale=float(HD) ** -0.5).then_inc(exp_done, 1)

            def evac_ot(g):
                if not g.real:
                    return
                if positive(g.n):
                    act.wait_ge(o_done, g.n)
                act.wait_ge(v2_free, g.n + 3)
                nc.scalar.copy(ot[:], out_ps[:, 0:KE * GT].rearrange("p (k t) -> p k t", k=KE)).then_inc(ot_evac, 1)

            def evac_x1t(g):
                if not g.real:
                    return
                act.wait_ge(x1t_done, g.n + 1)
                nc.scalar.copy(x1t[:, g.buf], emb_ps[:, 0:KE * GT].rearrange("p (k t) -> p k t", k=KE)).then_inc(x1t_evac, 1)

            def evac_qkt(g):
                if not g.real:
                    return
                act.wait_ge(qkt_done, g.n + 1)
                for a in range(KE):
                    nc.scalar.activation(qm[:, a].rearrange("p (i c) -> p i c", i=GI)[:, :, 0:TOK],
                                         emb_ps[:, a * GT:(a + 1) * GT].rearrange("p (i t) -> p i t", i=GI),
                                         ACT.Identity, bias=lnp[:, 1:2], scale=lnp[:, 0:1]).then_inc(qkt_evac, 1) if a == KE - 1 else \
                        nc.scalar.activation(qm[:, a].rearrange("p (i c) -> p i c", i=GI)[:, :, 0:TOK],
                                             emb_ps[:, a * GT:(a + 1) * GT].rearrange("p (i t) -> p i t", i=GI),
                                             ACT.Identity, bias=lnp[:, 1:2], scale=lnp[:, 0:1])
                for p in range(2):
                    nc.scalar.activation(k2[:, :, p], emb_ps[:, KE * GT:2 * KE * GT].rearrange("p (a t) -> p a t", a=KE),
                                         ACT.Identity, bias=klnb[:, p:p + 1], scale=klnw[:, p:p + 1]).then_inc(qkt_evac, 1)

            def squares(g):
                if not g.real:
                    return
                act.wait_ge(qk_ready, g.n + 1)
                if positive(g.n):
                    act.wait_ge(ss_done, g.n)
                nc.scalar.activation(sq[0:GT], qk[0:GT, g.buf], ACT.Square).then_inc(sq_done, 1)

            def high_x2(g):
                if not g.real:
                    return
                act.wait_ge(x2t_done, g.n + 1)
                nc.scalar.copy(x2hi[:, :, bass.ds(g.n * GT, GT)], out_ps[:, 0:KE * GT].rearrange("p (k t) -> p k t", k=KE)).then_inc(x2hi_done, 1)

            def slot(i, s):
                load_xs(Group(i, s + 2))
                evac_pt(Group(i, s - 1))
                exponentials(Group(i, s))
                evac_ot(Group(i, s - 1))
                evac_x1t(Group(i, s + 2))
                evac_qkt(Group(i, s + 1))
                squares(Group(i, s + 2))
                high_x2(Group(i, s - 1))

            slots(act, slot)

            for b in range(3 * FW_SETS // FW_BATCH):
                act.wait_ge(fwt_done, b + 1)
                w, n = divmod(b * FW_BATCH, FW_SETS)
                src = score_ps[:, b % 2].bitcast(F16)[:, 0:FW_BATCH * P]
                if w < 2:
                    m = n // KE
                    dst = (wgt, wut)[w].rearrange("p k (m c) -> p m k c", c=P)[:, m:m + FW_BATCH // KE]
                    src = src.rearrange("p (m k c) -> p m k c", k=KE, c=P)
                else:
                    for q in range(FW_BATCH):
                        k, m = divmod(n + q, MT)
                        cp = nc.scalar.copy(wdt[:, m, k * P:(k + 1) * P], src[:, q * P:(q + 1) * P])
                    cp.then_inc(fwt_evac, 1)
                    continue
                nc.scalar.copy(dst, src).then_inc(fwt_evac, 1)

            def chunk(c, groups):
                T = groups * GT
                for m in range(MT):
                    n = c * MT + m
                    act.wait_ge(gu_done, n + 1)
                    if positive(n - 1):
                        act.wait_ge(hf_done, n - 1)
                    nc.scalar.activation(sil[:, m % 2, 0:T], score_ps[:, m % 2, 0:T], ACT.Silu, scale=QUANT / XSCALE).then_inc(silu_done, 1)
                    act.wait_ge(hf_done, n + 1)
                    if positive(n - 1):
                        act.wait_ge(down_done, n - 1)
                    nc.scalar.copy(hhi[:, m % 2, 0:T], hf[:, m % 2, 0:T]).then_inc(hhi_done, 1)

            chunk(0, CG)
            with act.Fori(1, NCH) as c:
                chunk(c, CG)
            chunk(NCH, NG - NCH * CG)

        @block.vector
        def _(dve):
            dve.wait_ge(ident_ready, 1)
            nc.vector.tensor_copy(ident16[:], ident[:]).then_inc(ident16_ready, 1)
            for p in range(2):
                cols = ident.rearrange("p (j q d) -> p j q d", q=2, d=HD)[:, :, p]
                nc.vector.tensor_reduce(par[:, p:p + 1], cols, AX.XY, ALU.add).then_inc(par_ready, 1)
            n = 0
            for t in range(XTILES):
                dve.wait_ge(x_loaded[t], 16 * CH)
                for f in range(KF):
                    if t > 0:
                        dve.wait_ge(xt_done, XT_BATCHES * (t - 1) + 2 * (f + 1))
                    nc.vector.tensor_copy(xcut[0:XROWS, f // 2, f % 2].rearrange("p w (a b) -> p a w b", b=PATCH),
                                          xrow[0:XROWS, t, f // 2, (f % 2) * HALF:(f % 2 + 1) * HALF]).then_inc(xcut_ready, 1)
                for f in range(KF):
                    for w0 in range(0, GRID, XT_WP):
                        if n % 2 == 1:
                            dve.wait_ge(xt_done, n + 1)
                            nc.vector.tensor_copy(
                                xpt[:, f, t * XIMG:(t + 1) * XIMG, 2:TOK].rearrange("p b (hp wp) -> p wp b hp", wp=GRID)[:, w0:w0 + XT_WP],
                                score_ps[:, n % HG, 0:XT_WP * XROWS].rearrange("p (wp b hp) -> p wp b hp", wp=XT_WP, b=XIMG),
                            ).then_inc(xt_evac_dve, 1)
                        n += 1
                if t == 0:
                    dve.wait_ge(wt_evac, 4)
                    for k in range(KE):
                        nc.vector.tensor_reduce(wmean[:, k], wqkv[:, k, 0:2 * EMB].rearrange("p (h d) -> p h d", d=HD), AX.X, ALU.add).then_inc(means_done, 1)
                    for k in range(KE):
                        view = wqkv[:, k, 0:2 * EMB].rearrange("p (h d) -> p h d", d=HD)
                        dve.wait_ge(means_done, KE + k if k else KE)
                        nc.vector.tensor_scalar(wmean[:, k], wmean[:, k], 1.0 / HD, None, ALU.mult).then_inc(means_done, 1)
                        dve.wait_ge(means_done, KE + k + 1)
                        nc.vector.tensor_tensor(view, view, wmean[:, k].unsqueeze(2).to_broadcast([P, 2 * HEADS, HD]), ALU.subtract).then_inc(qkv_w_centred, 1)
            dve.wait_ge(rows_loaded, 16 * (4 * GI + 2))
            bview = bqkv[0:GT, 0:2 * EMB].rearrange("p (h d) -> p h d", d=HD)
            nc.vector.tensor_reduce(bmean[0:GT], bview, AX.X, ALU.add).then_inc(bmeans_done, 1)
            nc.vector.tensor_tensor(tok_add[0:GT], tok_add[0:GT], tok_pos[0:GT], ALU.add).then_inc(tok_added, 1)
            dve.wait_ge(bmeans_done, 1)
            nc.vector.tensor_scalar(bmean[0:GT], bmean[0:GT], 1.0 / HD, None, ALU.mult).then_inc(bmeans_done, 1)
            dve.wait_ge(bmeans_done, 2)
            nc.vector.tensor_tensor(bview, bview, bmean[0:GT].unsqueeze(2).to_broadcast([GT, 2 * HEADS, HD]), ALU.subtract).then_inc(qkv_w_centred, 1)
            dve.wait_ge(cols_loaded, 16 * 4)
            dve.wait_ge(par_ready, 2)
            nc.vector.tensor_scalar(klnw[:], par[:], lnp[:, 2:3], None, ALU.mult)
            nc.vector.tensor_scalar(klnb[:], par[:], lnp[:, 3:4], None, ALU.mult).then_inc(kln_ready, 1)
            for w in range(3):
                dve.wait_ge(ffn_loaded[w], 16)
                nc.vector.tensor_copy(w16[:, w], wraw[:, w]).then_inc(w16_ready, 1)
            dve.wait_ge(tok_added, 1)
            dve.wait_ge(qkv_w_centred, 3)

            def shift_scores(g):
                if not g.real:
                    return
                view = score_ps[0:GT, :, 0:KE * PAIR].rearrange("p j (h k) -> p j h k", k=TOK)
                dve.wait_ge(scores_done, g.n + 1)
                nc.vector.tensor_reduce(smax[0:GT, g.buf].rearrange("p (j h) -> p j h", j=HG), view, AX.X, ALU.max).then_inc(max_done, 1)
                dve.wait_ge(max_done, g.n + 1)
                if positive(g.n - 1):
                    dve.wait_ge(pt_done, 2 * (g.n - 1))
                nc.vector.tensor_tensor(prob[0:GT, g.buf], view,
                                        smax[0:GT, g.buf].rearrange("p (j h) -> p j h", j=HG).unsqueeze(3).to_broadcast([GT, HG, 4, TOK]),
                                        ALU.subtract).then_inc(sub_done, 1)

            def embed_tokens(g):
                if not g.real:
                    return
                dve.wait_ge(emb_done, g.n + 1)
                if positive(g.n - 1):
                    dve.wait_ge(res_ready, g.n - 1)
                nc.vector.tensor_tensor(h_emb[0:GT, g.buf], emb_ps[0:GT, 0:EMB], tok_add[0:GT], ALU.add).then_inc(h_ready, 1)
                dve.wait_ge(h_ready, g.n + 1)
                nc.vector.bn_stats(stats1[0:GT, g.buf], h_emb[0:GT, g.buf]).then_inc(stats1_done, 1)

            def token_variance(g):
                if not g.real:
                    return
                nc.vector.bn_aggr(mv1[0:GT, g.buf], stats1[0:GT, g.buf]).then_inc(mv1_done, 1)
                dve.wait_ge(mv1_done, g.n + 1)
                nc.vector.tensor_scalar(ve1[0:GT, g.buf:g.buf + 1], mv1[0:GT, g.buf, 1:2], LN_EPS, None, ALU.add).then_inc(ve1_done, 1)

            def sum_probs(g):
                if not g.real:
                    return
                dve.wait_ge(exp_done, g.n + 1)
                nc.vector.tensor_reduce(ssum[0:GT, g.buf], prob[0:GT, g.buf].rearrange("p j h k -> p (j h) k"), AX.X, ALU.add).then_inc(sum_done, 1)

            def invert_sums(g):
                if not g.real:
                    return
                nc.vector.reciprocal(rsum[0:GT, g.buf], ssum[0:GT, g.buf]).then_inc(rsum_done, 1)

            def norm_tokens(g):
                if not g.real:
                    return
                dve.wait_ge(rstd1_done, g.n + 1)
                if positive(g.n - 1):
                    dve.wait_ge(x1t_done, g.n - 1)
                nc.vector.tensor_scalar(xn1[0:GT, g.buf], h_emb[0:GT, g.buf], mv1[0:GT, g.buf, 0:1], rstd1[0:GT, g.buf:g.buf + 1],
                                        ALU.subtract, ALU.mult).then_inc(xn1_done, 1)

            def add_attention(g):
                if not g.real:
                    return
                dve.wait_ge(o_done, g.n + 1)
                dve.wait_ge(res_ready, g.n + 1)
                if positive(g.n):
                    dve.wait_ge(h2_kept, g.n)
                nc.vector.tensor_tensor(hcur[0:GT], out_ps[0:GT, 0:EMB], h2[0:GT, g.n], ALU.add).then_inc(h2_ready, 1)
                dve.wait_ge(h2_ready, g.n + 1)
                nc.vector.bn_stats(stats2[0:GT], hcur[0:GT]).then_inc(stats2_done, 1)

            def residual_variance(g):
                if not g.real:
                    return
                nc.vector.bn_aggr(mv2[0:GT], stats2[0:GT]).then_inc(mv2_done, 1)
                dve.wait_ge(mv2_done, g.n + 1)
                nc.vector.tensor_scalar(ve2[0:GT], mv2[0:GT, 1:2], LN_EPS, XSCALE ** -2, ALU.add, ALU.mult).then_inc(ve2_done, 1)

            def norm_residual(g):
                if not g.real:
                    return
                dve.wait_ge(rstd2_done, g.n + 1)
                nc.vector.tensor_scalar(xn2[0:GT], hcur[0:GT], mv2[0:GT, 0:1], rstd2[0:GT], ALU.subtract, ALU.mult).then_inc(xn2_done, 1)

            def bias_qkv(g):
                if not g.real:
                    return
                dve.wait_ge(qkv_done, g.n + 1)
                if positive(g.n - 1):
                    dve.wait_ge(qkt_done, g.n - 1)
                nc.vector.tensor_tensor(qk[0:GT, g.buf], ptq_ps0[0:GT], bqkv[0:GT, 0:2 * EMB], ALU.add).then_inc(qk_ready, 1)
                if positive(g.turn):
                    dve.wait_ge(v_moved[g.buf], 16 * 2 * GI * g.turn)
                nc.vector.tensor_tensor(vt[0:GT, g.buf].rearrange("p q d c -> p q c d"), ptq_ps1[0:GT, 0:EMB].rearrange("p (c q d) -> p q c d", q=2, d=HD),
                                        bqkv[0:GT, 2 * EMB:QKV].rearrange("p (c q d) -> p q c d", q=2, d=HD), ALU.add).then_inc(v_ready, 1)

            def variance_qk(g):
                if not g.real:
                    return
                dve.wait_ge(sq_done, g.n + 1)
                nc.vector.tensor_reduce(ss[0:GT, g.buf], sq[0:GT].rearrange("p (h d) -> p h d", d=HD), AX.X, ALU.add).then_inc(ss_done, 1)
                dve.wait_ge(ss_done, g.n + 1)
                if positive(g.n):
                    dve.wait_ge(rstd_qk_done, g.n)
                nc.vector.tensor_scalar(ve_qk[0:GT], ss[0:GT, g.buf], 1.0 / HD, LN_EPS, ALU.mult, ALU.add).then_inc(ve_qk_done, 1)

            def low_x2(g):
                if not g.real:
                    return
                dve.wait_ge(x2hi_done, g.n + 1)
                nc.vector.tensor_tensor(x2lo[:, :, bass.ds(g.n * GT, GT)], out_ps[:, 0:KE * GT].rearrange("p (k t) -> p k t", k=KE),
                                        x2hi[:, :, bass.ds(g.n * GT, GT)], ALU.subtract).then_inc(x2lo_done, 1)

            def slot(i, s):
                shift_scores(Group(i, s))
                embed_tokens(Group(i, s + 2))
                embedded, attended = Group(i, s + 2), Group(i, s - 1)
                if embedded.real:
                    dve.wait_ge(stats1_done, embedded.n + 1)
                sum_probs(Group(i, s))
                token_variance(embedded)
                norm_tokens(embedded)
                add_attention(attended)
                if attended.real:
                    dve.wait_ge(stats2_done, attended.n + 1)
                if Group(i, s).real:
                    dve.wait_ge(sum_done, Group(i, s).n + 1)
                invert_sums(Group(i, s))
                residual_variance(attended)
                norm_residual(Group(i, s - 1))
                bias_qkv(Group(i, s + 2))
                low_x2(Group(i, s - 1))
                variance_qk(Group(i, s + 2))

            slots(dve, slot)
            dve.wait_ge(h2_kept, NG)

            acc = (ptq_ps0, ptq_ps1, out_ps)

            def chunk(c, groups):
                T = groups * GT
                for m in range(MT):
                    n = c * MT + m
                    dve.wait_ge(silu_done, n + 1)
                    if positive(n - 1):
                        dve.wait_ge(hhi_done, n - 1)
                    nc.vector.scalar_tensor_tensor(out=hf[:, m % 2, 0:T], in0=score_ps[:, 2 + m % 2, 0:T], scalar=QUANT / XSCALE * HSCALE,
                                                   in1=sil[:, m % 2, 0:T], op0=ALU.mult, op1=ALU.mult).then_inc(hf_done, 1)
                    dve.wait_ge(hhi_done, n + 1)
                    nc.vector.tensor_tensor(hlo[:, m % 2, 0:T], hf[:, m % 2, 0:T], hhi[:, m % 2, 0:T], ALU.subtract).then_inc(hlo_done, 1)
                dve.wait_ge(down_done, (c + 1) * MT)
                for q in range(groups):
                    row = h2[0:GT, c * CG + q]
                    nc.vector.scalar_tensor_tensor(out=row, in0=acc[q][0:GT, 0:EMB], scalar=QUANT / HSCALE,
                                                   in1=row, op0=ALU.mult, op1=ALU.add).then_inc(y_ready, 1)

            chunk(0, CG)
            with dve.Fori(1, NCH) as c:
                chunk(c, CG)
            chunk(NCH, NG - NCH * CG)


_INS = ["x", "cls_tok", "L0_tok_W", "L0_tok_b", "L0_tok_cls_token", "L0_tok_pos_emb", "L0_attn_qkv_w", "L0_attn_qkv_b",
        "L0_attn_o_w", "L0_attn_o_b", "L0_attn_q_norm_w", "L0_attn_q_norm_b", "L0_attn_k_norm_w", "L0_attn_k_norm_b",
        "L0_ffn_w_gate", "L0_ffn_w_up", "L0_ffn_w_down"]


def kernel(**inputs):
    import numpy as _np
    import concourse.bacc as _bacc
    from concourse.bass_utils import run_bass_kernel_spmd as _run

    nc = _bacc.Bacc("TRN2", target_bir_lowering=False, num_devices=1)
    arrays, args = {}, []
    for name in _INS:
        a = _np.ascontiguousarray(inputs[name])
        arrays[f"in_{name}"] = a
        args.append(nc.dram_tensor(f"in_{name}", a.shape, mybir.dt.from_np(a.dtype), kind="ExternalInput").ap())
    args.append(nc.dram_tensor("out_0", (IMAGES, TOK, EMB), F32, kind="ExternalOutput").ap())
    vit_kernel(nc, *args)
    r = _run(nc, [arrays], core_ids=[0])
    return r.results[0]["out_0"]
```

```python
from contextlib import ExitStack

import concourse.bass as bass
from concourse import mybir
from concourse.alu_op_type import AluOpType as ALU

ACT = mybir.ActivationFunctionType
F32 = mybir.dt.float32
F16 = mybir.dt.float16
I32 = mybir.dt.int32
AX = mybir.AxisListType

P = 128
BANK = 512

IMAGES, CH, SIDE, PATCH = 32, 3, 96, 16
GRID = SIDE // PATCH
EMB = 256
KE = EMB // P
TOK = GRID * GRID + 2
TABLE = TOK + 2
FEAT = CH * PATCH * PATCH
KF = FEAT // P
HALF = PATCH // 2

GI = 3
GT = GI * TOK
NG = -(-IMAGES // GI)
LAST_ROWS = (IMAGES - GI * (NG - 1)) * TOK
XIMG = 16
XROWS = XIMG * GRID
XTILES = IMAGES // XIMG

HEADS, HD = 16, 16
QKV = 3 * EMB
HG = 2
HR = P // HG // HD
PAIR = 2 * TOK
NPAIR = HEADS // 2
HID = 768
MT = HID // P
CG = 2
NCH = -(-NG // CG)
LN_EPS = 1e-5
RSQRT_MAGIC = float(0x5F3759DF)
NEWTON_TURNS = 3
FFN_SLOT = 3
NEWTON_OPS = 3 * NEWTON_TURNS + 1
QUANT = 1.0 / 127.0
XSCALE = 2.0 ** 11
HSCALE = 2.0 ** -3


class Group:

    def __init__(self, i, c):
        self.n = 2 * i + c
        self.buf = c % 2
        self.turn = i + c // 2
        self.real = not isinstance(self.n, int) or 0 <= self.n < NG


class Chunk:

    def __init__(self, i, s):
        self.n = i + (s - FFN_SLOT) // 2
        known = isinstance(self.n, int)
        self.real = not known or 0 <= self.n < NCH
        self.groups = min(CG, NG - CG * self.n) if known else CG


def positive(n):
    return not isinstance(n, int) or n > 0


def vit_kernel(nc, x, cls_tok, w_emb, b_emb, cls_token, pos_emb, qkv_w, qkv_b, o_w, o_b,
               qn_w, qn_b, kn_w, kn_b, w_gate, w_up, w_down, out):
    with ExitStack() as ctx:
        def sb(name, shape, dt=F32):
            return ctx.enter_context(nc.sbuf_tensor(name, shape, dt))

        def sem(name):
            return ctx.enter_context(nc.semaphore(name))

        ident = sb("ident", [P, P])
        ident16 = sb("ident16", [P, P], F16)
        xrow = sb("xrow", [P, XTILES, CH, PATCH, GRID, PATCH])
        xcut = sb("xcut", [P, CH, 2, GRID, HALF * PATCH])
        xpt = sb("xpt", [P, KF, (NG + 1) * GI, TOK])
        xs = sb("xs", [P, 2, KF, GT])
        wemb = sb("wemb", [P, CH, 2, EMB])
        wqkv_raw = sb("wqkv_raw", [P, QKV // P, EMB])
        wqkv = sb("wqkv", [P, KE, QKV])
        wo_raw = sb("wo_raw", [P, KE, EMB])
        wo = sb("wo", [P, KE, EMB])
        wmean = sb("wmean", [P, KE, 2 * HEADS])
        bqkv = sb("bqkv", [P, QKV])
        bmean = sb("bmean", [P, 2 * HEADS])
        bo = sb("bo", [P, EMB])
        row_table = sb("row_table", [TABLE, EMB])
        row_sel = sb("row_sel", [TABLE, GT])
        tok_add = sb("tok_add", [P, EMB])
        lnp = sb("lnp", [P, 4])
        par = sb("par", [P, HR])
        klnw = sb("klnw", [P, HR])
        klnb = sb("klnb", [P, HR])
        mhalf = sb("mhalf", [P, 1])

        h_emb = sb("h_emb", [P, 2, EMB])
        stats1 = sb("stats1", [P, 2, 6])
        mv1 = sb("mv1", [P, 2, 2])
        ve1 = sb("ve1", [P, 2])
        rstd1 = sb("rstd1", [P, 2])
        xn1 = sb("xn1", [P, 2, EMB])
        x1t = sb("x1t", [P, 2, KE, GT])
        qk = sb("qk", [P, 2, 2 * EMB])
        sq = sb("sq", [P, 2 * EMB])
        ss = sb("ss", [P, 2, 2 * HEADS])
        ve_qk = sb("ve_qk", [P, 2 * HEADS])
        rstd_qk = sb("rstd_qk", [P, 2, 2 * HEADS])
        newton = sb("newton", [P, 2 * HEADS])
        vt = sb("vt", [P, 2, 2, HD, HEADS // 2])
        v2 = sb("v2", [PAIR, 2, GI, 2 * HD, HEADS // 2])
        qm = sb("qm", [P, KE, GI * (GT + TOK)])
        k2 = sb("k2", [P, KE, HR, GT])
        prob = sb("prob", [P, 2, HG, KE * HR, TOK])
        smax = sb("smax", [P, 2, HEADS])
        ssum = sb("ssum", [P, 2, HEADS])
        rsum = sb("rsum", [P, 2, HEADS])
        pt = sb("pt", [PAIR, NPAIR, GT])
        ot = sb("ot", [P, KE, GT])
        h2 = sb("h2", [P, NG, EMB])
        hcur = sb("hcur", [P, EMB])
        stats2 = sb("stats2", [P, 6])
        mv2 = sb("mv2", [P, 2])
        ve2 = sb("ve2", [P, 1])
        rstd2 = sb("rstd2", [P, 1])
        xn2 = sb("xn2", [P, EMB])
        x2hi = sb("x2hi", [P, KE, NG * GT], F16)
        x2lo = sb("x2lo", [P, KE, NG * GT], F16)

        wraw = xrow.rearrange("p t c a w b -> p t (c a w b)")[:, 0].bitcast(I32).rearrange("p (n e) -> p n e", n=3)
        w16 = sb("w16", [P, 3, MT * EMB], F16)
        wgt = sb("wgt", [P, KE, HID], F16)
        wut = sb("wut", [P, KE, HID], F16)
        wdt = sb("wdt", [P, MT, EMB], F16)
        th = sb("th", [P, 2, CG * GT])
        gated = sb("gated", [P, 2, CG * GT])
        hf = sb("hf", [P, 2, CG * GT])
        hhi = sb("hhi", [P, 2, CG * GT], F16)
        hlo = sb("hlo", [P, 2, CG * GT], F16)

        def bank(name):
            return ctx.enter_context(nc.psum_tensor(name, [P, BANK], F32))

        score_ps = ctx.enter_context(nc.psum_tensor("score_ps", [P, HG, BANK], F32))
        spare_ps = ctx.enter_context(nc.psum_tensor("spare_ps", [P, 2, BANK], F32))
        gu_ps, acc_ps = spare_ps[:, 0], spare_ps[:, 1]
        ptq_ps0, ptq_ps1, out_ps, emb_ps = bank("ptq_ps0"), bank("ptq_ps1"), bank("out_ps"), bank("emb_ps")
        x_banks = [score_ps[:, 0], score_ps[:, 1], spare_ps[:, 0], spare_ps[:, 1]]

        x_loaded = [[sem(f"x_loaded{t}_{c}") for c in range(CH)] for t in range(XTILES)]
        wemb_loaded, wqkv_loaded, wo_loaded = sem("wemb_loaded"), sem("wqkv_loaded"), sem("wo_loaded")
        ffn_loaded = [sem(f"ffn_loaded{i}") for i in range(3)]
        rows_loaded, cols_loaded = sem("rows_loaded"), sem("cols_loaded")
        ident_zero, ident_ready, ident16_ready = sem("ident_zero"), sem("ident_ready"), sem("ident16_ready")
        table_loaded, sel_zero, sel_ready, tok_turned = sem("table_loaded"), sem("sel_zero"), sem("sel_ready"), sem("tok_turned")
        xpt_zeroed, qm_zeroed = sem("xpt_zeroed"), sem("qm_zeroed")
        mhalf_ready = sem("mhalf_ready")
        par_ready, tok_added, qkv_w_centred = sem("par_ready"), sem("tok_added"), sem("qkv_w_centred")
        means_done, bmeans_done, kln_ready = sem("means_done"), sem("bmeans_done"), sem("kln_ready")
        xcut_ready = [sem(f"xcut_ready{t}") for t in range(XTILES)]
        xt_done, xt_evac_act, xt_evac_dve = sem("xt_done"), sem("xt_evac_act"), sem("xt_evac_dve")
        wt_done, wt_evac = sem("wt_done"), sem("wt_evac")

        xs_loaded = [sem(f"xs_loaded{b}") for b in range(2)]
        v_moved = [sem(f"v_moved{b}") for b in range(2)]
        emb_done, x1t_done, qkv_done = sem("emb_done"), sem("x1t_done"), sem("qkv_done")
        qkt_done, scores_done, pt_done = sem("qkt_done"), sem("scores_done"), sem("pt_done")
        v2_free, o_done, x2t_done = sem("v2_free"), sem("o_done"), sem("x2t_done")
        h_ready, stats1_done, mv1_done, ve1_done = sem("h_ready"), sem("stats1_done"), sem("mv1_done"), sem("ve1_done")
        rstd1_done, xn1_done = sem("rstd1_done"), sem("xn1_done")
        res_ready, x1t_evac = sem("res_ready"), sem("x1t_evac")
        qk_ready, v_ready, sq_done, ss_done = sem("qk_ready"), sem("v_ready"), sem("sq_done"), sem("ss_done")
        newton_done = sem("newton_done")
        ve_qk_done, rstd_qk_done, qkn_done, qkt_evac = sem("ve_qk_done"), sem("rstd_qk_done"), sem("qkn_done"), sem("qkt_evac")
        max_done, sub_done, exp_done, sum_done = sem("max_done"), sem("sub_done"), sem("exp_done"), sem("sum_done")
        rsum_done, probs_ready, pt_evac, ot_evac = sem("rsum_done"), sem("probs_ready"), sem("pt_evac"), sem("ot_evac")
        h2_kept = sem("h2_kept")
        h2_ready, stats2_done, mv2_done, ve2_done = sem("h2_ready"), sem("stats2_done"), sem("mv2_done"), sem("ve2_done")
        rstd2_done, xn2_done, x2hi_done, x2lo_done = sem("rstd2_done"), sem("xn2_done"), sem("x2hi_done"), sem("x2lo_done")

        w16_ready, fwt_done, fwt_evac = sem("w16_ready"), sem("fwt_done"), sem("fwt_evac")
        gu_free, gu_done, tanh_done, gated_done = sem("gu_free"), sem("gu_done"), sem("tanh_done"), sem("gated_done")
        hhi_done, hlo_done, down_done = sem("hhi_done"), sem("hlo_done"), sem("down_done")
        acc_free, y_stored = sem("acc_free"), sem("y_stored")

        out_rows = out.rearrange("b t e -> (b t) e")
        FW_SETS = MT * KE
        FW_BATCH = 4
        QKT_EVACS = 1 + HR
        XT_WP = 3
        XT_BATCHES = KF * (GRID // XT_WP)
        W_BATCHES = (QKV // P) * KE // 4 + KE * KE // 4

        AHEAD, BEHIND = 2, 2
        steady = (NG - AHEAD - FFN_SLOT) // 2
        def x_bank(n):
            return x_banks[n % 4] if n < XT_BATCHES else x_banks[2 + n % 2]

        def slots(eng, run_slot):
            for s in range(-AHEAD, FFN_SLOT):
                run_slot(0, s)
            with eng.Fori(0, steady) as i:
                run_slot(i, FFN_SLOT)
                run_slot(i, FFN_SLOT + 1)
            for s in range(FFN_SLOT + 2 * steady, FFN_SLOT + 2 * NCH):
                run_slot(0, s)

        def x_bank_free(eng, n):
            used = n - 4 if n < XT_BATCHES else n - 2
            if used >= XT_BATCHES:
                eng.wait_ge(xt_evac_act, used + 1 - XT_BATCHES // 2)
            elif used >= 0:
                eng.wait_ge(xt_evac_dve if used % 2 else xt_evac_act, used // 2 + 1)

        def x_turned(n):
            return x_bank(n)[:, 0:XT_WP * XROWS].rearrange("p (wp b hp) -> p wp b hp", wp=XT_WP, b=XIMG)

        def x_patches(n):
            t, f, w0 = n // XT_BATCHES, n % XT_BATCHES // (GRID // XT_WP), n % (GRID // XT_WP) * XT_WP
            tokens = xpt[:, f, t * XIMG:(t + 1) * XIMG, 2:TOK]
            return tokens.rearrange("p b (hp wp) -> p wp b hp", wp=GRID)[:, w0:w0 + XT_WP]

        block = ctx.enter_context(nc.Block())

        @block.sync
        def _(sp):
            x_dram = x.rearrange("b c (hp p1) w -> b hp c (p1 w)", p1=PATCH)
            xrow_flat = xrow.rearrange("p t c a w b -> p t c (a w b)")

            def load_x(t):
                for c in range(CH):
                    sp.dma_start(xrow_flat[0:XROWS, t, c], x_dram[t * XIMG:(t + 1) * XIMG, :, c]).then_inc(x_loaded[t][c], 16)

            load_x(0)
            w_dram = w_emb.rearrange("(h p c) e -> p h (c e)", h=2, p=P)
            for hh in range(2):
                sp.dma_start(wemb[:, :, hh, :], w_dram[:, hh].rearrange("p (c e) -> p c e", c=CH)).then_inc(wemb_loaded, 16)
            sp.dma_start(wqkv_raw[:], qkv_w.rearrange("(t p) k -> p t k", p=P)).then_inc(wqkv_loaded, 16)
            sp.dma_start(row_table[0:1], cls_tok.rearrange("a b e -> (a b) e")).then_inc(table_loaded, 16)
            sp.dma_start(row_table[1:TOK], pos_emb).then_inc(table_loaded, 16)
            sp.dma_start(row_table[TOK:TOK + 1], cls_token.rearrange("a b e -> (a b) e")).then_inc(table_loaded, 16)
            sp.dma_start(row_table[TOK + 1:TABLE], b_emb.rearrange("(a e) -> a e", a=1)).then_inc(table_loaded, 16)
            sp.dma_start(wo_raw[:], o_w.rearrange("(t p) k -> p t k", p=P)).then_inc(wo_loaded, 16)
            sp.dma_start(bqkv[0:GT], qkv_b.partition_broadcast(GT)).then_inc(rows_loaded, 16)
            sp.dma_start(bo[0:GT], o_b.partition_broadcast(GT)).then_inc(rows_loaded, 16)
            sp.wait_ge(xt_evac_act, XT_BATCHES // 2)
            sp.wait_ge(xt_evac_dve, XT_BATCHES // 2)
            load_x(1)
            for n, v in enumerate((qn_w, qn_b, kn_w, kn_b)):
                sp.dma_start(lnp[:, n:n + 1], v.partition_broadcast(P // HD).rearrange("r (d a) -> r d a", a=1)).then_inc(cols_loaded, 16)
            sp.wait_ge(xcut_ready[0], KF)
            for n, w in enumerate((w_gate, w_up)):
                sp.dma_start(wraw[:, n].rearrange("p (t k) -> p t k", t=MT), w.rearrange("(t p) k -> p t k", p=P)).then_inc(ffn_loaded[n], 16)
            sp.dma_start(wraw[:, 2].rearrange("p (t k) -> p t k", t=KE), w_down.rearrange("(t p) k -> p t k", p=P)).then_inc(ffn_loaded[2], 16)

            def move_v(g):
                if not g.real:
                    return
                count = g.n + 1
                sp.wait_ge(v_ready, count)
                sp.wait_ge(v2_free, count)
                for im in range(GI):
                    for hp in range(2):
                        sp.dma_start(v2[hp * TOK:(hp + 1) * TOK, g.buf, im, hp * HD:(hp + 1) * HD], vt[im * TOK:(im + 1) * TOK, g.buf, hp]).then_inc(v_moved[g.buf], 16)


            def slot(i, s):
                move_v(Group(i, s + 1))

            slots(sp, slot)

            for c in range(NCH):
                sp.wait_ge(acc_free, c + 2)
                for g in range(c * CG, min((c + 1) * CG, NG)):
                    rows = GT if g < NG - 1 else LAST_ROWS
                    sp.dma_start(out_rows[g * GT:g * GT + rows], h2[0:rows, g]).then_inc(y_stored, 16)
            sp.wait_ge(y_stored, 16 * NG)

        @block.gpsimd
        def _(pool):
            nc.gpsimd.memset(ident[:], 0.0).then_inc(ident_zero, 1)
            pool.wait_ge(ident_zero, 1)
            nc.gpsimd.affine_select(out=ident[:], in_=ident[:], compare_op=ALU.not_equal, fill=1.0, base=0,
                                    pattern=[[-1, P]], channel_multiplier=1).then_inc(ident_ready, 1)
            nc.gpsimd.memset(row_sel[:], 0.0).then_inc(sel_zero, 1)
            images = [[0, GI], [1, TOK]]
            pool.wait_ge(sel_zero, 1)
            nc.gpsimd.affine_select(out=row_sel[:], in_=row_sel[:], compare_op=ALU.not_equal, fill=1.0, base=0,
                                    pattern=images, channel_multiplier=-1).then_inc(sel_zero, 1)
            pool.wait_ge(sel_zero, 2)
            nc.gpsimd.affine_select(out=row_sel[:], in_=row_sel[:], compare_op=ALU.not_equal, fill=1.0, base=-1 - P * TOK,
                                    pattern=images, channel_multiplier=P).then_inc(sel_zero, 1)
            pool.wait_ge(sel_zero, 3)
            nc.gpsimd.affine_select(out=row_sel[:], in_=row_sel[:], compare_op=ALU.is_gt, fill=1.0, base=2 + P * (TOK + 1),
                                    pattern=[[0, GI], [-1, TOK]], channel_multiplier=-P).then_inc(sel_ready, 1)
            nc.gpsimd.memset(xpt[:, :, IMAGES:(NG + 1) * GI, :], 0.0)
            nc.gpsimd.memset(xpt[:, :, 0:IMAGES, 0:2], 0.0).then_inc(xpt_zeroed, 1)
            nc.gpsimd.memset(mhalf[:], -0.5).then_inc(mhalf_ready, 1)
            nc.gpsimd.memset(qm[:], 0.0).then_inc(qm_zeroed, 1)
            for b in range(2):
                nc.gpsimd.memset(v2[:, b], 0.0).then_inc(v2_free, 1)

            pool.wait_ge(rows_loaded, 16 * 2)
            pool.wait_ge(mhalf_ready, 1)

            def residual(g):
                if not g.real:
                    return
                pool.wait_ge(h_ready, g.n + 1)
                nc.gpsimd.tensor_tensor(h2[0:GT, g.n], h_emb[0:GT, g.buf], bo[0:GT], ALU.add).then_inc(res_ready, 1)

            def rstd_of_tokens(g):
                if not g.real:
                    return
                pool.wait_ge(ve1_done, g.n + 1)
                nc.gpsimd.tensor_tensor(rstd1[0:GT, g.buf:g.buf + 1], ve1[0:GT, g.buf:g.buf + 1],
                                        mhalf[0:GT], ALU.pow).then_inc(rstd1_done, 1)

            def rstd_of_residual(g):
                if not g.real:
                    return
                pool.wait_ge(ve2_done, g.n + 1)
                nc.gpsimd.tensor_tensor(rstd2[0:GT], ve2[0:GT], mhalf[0:GT], ALU.pow).then_inc(rstd2_done, 1)

            def keep_residual(g):
                if not g.real:
                    return
                pool.wait_ge(h2_ready, g.n + 1)
                nc.gpsimd.tensor_copy(h2[0:GT, g.n], hcur[0:GT]).then_inc(h2_kept, 1)

            def norm_qk(g):
                if not g.real:
                    return
                pool.wait_ge(rstd_qk_done, g.n + 1)
                view = qk[0:GT, g.buf].rearrange("p (h d) -> p h d", d=HD)
                nc.gpsimd.tensor_tensor(view, view, rstd_qk[0:GT, g.buf].unsqueeze(2).to_broadcast([GT, 2 * HEADS, HD]),
                                        ALU.mult).then_inc(qkn_done, 1)

            def norm_probs(g):
                if not g.real:
                    return
                pool.wait_ge(rsum_done, g.n + 1)
                view = prob[0:GT, g.buf].rearrange("p j h k -> p (j h) k")
                nc.gpsimd.tensor_tensor(view, view, rsum[0:GT, g.buf].unsqueeze(2).to_broadcast([GT, HEADS, TOK]),
                                        ALU.mult).then_inc(probs_ready, 1)

            def low_hidden(c, m):
                if not c.real:
                    return
                n, T = c.n * MT + m, c.groups * GT
                pool.wait_ge(hhi_done, n + 1)
                nc.gpsimd.tensor_tensor(hlo[:, m % 2, 0:T], hf[:, m % 2, 0:T], hhi[:, m % 2, 0:T], ALU.subtract).then_inc(hlo_done, 1)

            def slot(i, s):
                c, first = Chunk(i, s), s % 2 == 1
                rstd_of_tokens(Group(i, s + 2))
                residual(Group(i, s + 2))
                norm_qk(Group(i, s + 1))
                if first:
                    low_hidden(c, 0)
                    norm_probs(Group(i, s))
                    low_hidden(c, 1)
                    rstd_of_residual(Group(i, s - 1))
                    keep_residual(Group(i, s - 1))
                    low_hidden(c, 2)
                else:
                    low_hidden(c, 3)
                    low_hidden(c, 4)
                    norm_probs(Group(i, s))
                    low_hidden(c, 5)
                    rstd_of_residual(Group(i, s - 1))
                    keep_residual(Group(i, s - 1))

            slots(pool, slot)

        @block.tensor
        def _(pe):
            pe.wait_ge(ident_ready, 1)

            def turn_x(t, features):
                for f in features:
                    pe.wait_ge(xcut_ready[t], f + 1)
                    for w0 in range(0, GRID, XT_WP):
                        n = t * XT_BATCHES + f * (GRID // XT_WP) + w0 // XT_WP
                        x_bank_free(pe, n)
                        for w in range(XT_WP):
                            mm = pe.transpose(x_bank(n)[:, w * XROWS:(w + 1) * XROWS], xcut[0:XROWS, f // 2, f % 2, w0 + w],
                                              ident[0:XROWS, 0:XROWS])
                        mm.then_inc(xt_done, 1)

            turn_x(0, range(KF))
            pe.wait_ge(table_loaded, 16 * 4)
            pe.wait_ge(sel_ready, 1)
            pe.matmul(out_ps[0:GT, 0:EMB], row_sel[:], row_table[:], start=True, stop=True).then_inc(tok_turned, 1)
            pe.wait_ge(wqkv_loaded, 16)
            pe.wait_ge(wo_loaded, 16)
            m = 0
            for raw, tiles, step in ((wqkv_raw, QKV // P, 3), (wo_raw, KE, KE)):
                for k in range(KE):
                    for r0 in range(0, tiles, step):
                        if m >= 2:
                            pe.wait_ge(wt_evac, m - 1)
                        for r in range(step):
                            mm = pe.transpose((ptq_ps0, ptq_ps1)[m % 2][:, r * P:(r + 1) * P], raw[:, r0 + r, k * P:(k + 1) * P], ident[:])
                        mm.then_inc(wt_done, 1)
                        m += 1
            pe.wait_ge(wemb_loaded, 32)

            def embed(g):
                if not g.real:
                    return
                pe.wait_ge(xs_loaded[g.buf], 16 * (g.turn + 1))
                if positive(g.n - 1):
                    pe.wait_ge(qkt_evac, QKT_EVACS * (g.n - 1))
                for f in range(KF):
                    mm = pe.matmul(emb_ps[0:GT, 0:EMB], xs[:, g.buf, f], wemb[:, f // 2, f % 2], start=(f == 0), stop=(f == KF - 1))
                mm.then_inc(emb_done, 1)

            def turn_xn1(g):
                if not g.real:
                    return
                pe.wait_ge(xn1_done, g.n + 1)
                for k in range(KE):
                    mm = pe.transpose(emb_ps[:, k * GT:(k + 1) * GT], xn1[0:GT, g.buf, k * P:(k + 1) * P], ident[0:GT, 0:GT])
                mm.then_inc(x1t_done, 1)

            def project_qkv(g):
                if not g.real:
                    return
                pe.wait_ge(x1t_evac, g.n + 1)
                if positive(g.n - 2):
                    pe.wait_ge(pt_evac, 2 * (g.n - 2))
                for k in range(KE):
                    pe.matmul(ptq_ps0[0:GT], x1t[:, g.buf, k], wqkv[:, k, 0:2 * EMB], start=(k == 0), stop=(k == KE - 1))
                for k in range(KE):
                    mm = pe.matmul(ptq_ps1[0:GT, 0:EMB], x1t[:, g.buf, k], wqkv[:, k, 2 * EMB:QKV], start=(k == 0), stop=(k == KE - 1))
                mm.then_inc(qkv_done, 1)

            def turn_qk(g):
                if not g.real:
                    return
                pe.wait_ge(qkn_done, g.n + 1)
                if g.real and (not isinstance(g.n, int) or g.n + 1 < NG):
                    pe.wait_ge(x1t_evac, g.n + 2)
                for k in range(2 * KE):
                    mm = pe.transpose(emb_ps[:, k * GT:(k + 1) * GT], qk[0:GT, g.buf, k * P:(k + 1) * P], ident[0:GT, 0:GT])
                mm.then_inc(qkt_done, 1)

            def scores(g):
                if not g.real:
                    return
                pe.wait_ge(qkt_evac, QKT_EVACS * (g.n + 1))
                if positive(g.n):
                    pe.wait_ge(sub_done, g.n)
                for a in range(KE):
                    for im in range(GI):
                        for j in range(HG):
                            rows = slice(j * (P // HG), (j + 1) * (P // HG))
                            mm = pe.matmul(score_ps[0:GT, j, a * HR * TOK:(a + 1) * HR * TOK],
                                           qm[rows, a, im * GT:(im + 1) * GT],
                                           k2[rows, a, :, im * TOK:(im + 1) * TOK],
                                           start=(im == 0), stop=(im == GI - 1))
                mm.then_inc(scores_done, 1)

            def turn_probs(g):
                if not g.real:
                    return
                pe.wait_ge(probs_ready, g.n + 1)
                if not isinstance(g.n, int) or g.n + 2 < NG:
                    pe.wait_ge(qk_ready, g.n + 3)
                    pe.wait_ge(v_ready, g.n + 3)
                for c in range(NPAIR):
                    src = prob[0:GT, g.buf].rearrange("p j h k -> p (j h k)")[:, c * PAIR:(c + 1) * PAIR]
                    mm = pe.transpose((ptq_ps0, ptq_ps1)[c // 4][0:PAIR, (c % 4) * GT:(c % 4 + 1) * GT], src, ident[0:GT, 0:GT])
                    if c % 4 == 3:
                        mm.then_inc(pt_done, 1)

            def attend(g):
                if not g.real:
                    return
                pe.wait_ge(pt_evac, 2 * (g.n + 1))
                pe.wait_ge(v_moved[g.buf], 16 * 2 * GI * (g.turn + 1))
                if positive(g.n):
                    pe.wait_ge(x2lo_done, g.n)
                for a in range(KE):
                    for im in range(GI):
                        for c in range(NPAIR // KE):
                            at = (c // 2) * (2 * KE) + a * 2 + c % 2
                            mm = pe.matmul(out_ps[c * 32:(c + 1) * 32, a * GT + im * TOK:a * GT + (im + 1) * TOK],
                                           v2[:, g.buf, im, :, a * (NPAIR // KE) + c],
                                           pt[:, at, im * TOK:(im + 1) * TOK], start=True, stop=True)
                mm.then_inc(v2_free, 1)

            def project_out(g):
                if not g.real:
                    return
                pe.wait_ge(ot_evac, g.n + 1)
                for k in range(KE):
                    mm = pe.matmul(out_ps[0:GT, 0:EMB], ot[:, k], wo[:, k], start=(k == 0), stop=(k == KE - 1))
                mm.then_inc(o_done, 1)

            def turn_xn2(g):
                if not g.real:
                    return
                pe.wait_ge(xn2_done, g.n + 1)
                for k in range(KE):
                    mm = pe.transpose(out_ps[:, k * GT:(k + 1) * GT], xn2[0:GT, k * P:(k + 1) * P], ident[0:GT, 0:GT])
                mm.then_inc(x2t_done, 1)

            def gate_up(c, m):
                if not c.real:
                    return
                T = c.groups * GT
                if m == 0:
                    pe.wait_ge(x2lo_done, c.n * CG + c.groups)
                pe.wait_ge(gu_free, c.n * MT + m + 1)
                for u, w in enumerate((wgt, wut)):
                    for k in range(KE):
                        for part in (x2hi, x2lo):
                            mm = pe.matmul(gu_ps[:, u * T:(u + 1) * T], w[:, k, m * P:(m + 1) * P], part[:, k, bass.ds(c.n * (CG * GT), T)],
                                           start=(k == 0 and part is x2hi), stop=(k == KE - 1 and part is x2lo))
                mm.then_inc(gu_done, 1)

            def down(c, m):
                if not c.real:
                    return
                pe.wait_ge(hhi_done, c.n * MT + m + 1)
                pe.wait_ge(hlo_done, c.n * MT + m + 1)
                if m == 0:
                    pe.wait_ge(acc_free, c.n + 1)
                for q in range(c.groups):
                    for part in (hhi, hlo):
                        mm = pe.matmul(acc_ps[0:GT, q * EMB:(q + 1) * EMB], part[:, m % 2, q * GT:(q + 1) * GT], wdt[:, m],
                                       start=(m == 0 and q == 0 and part is hhi), stop=(m == MT - 1 and part is hlo), skip_group_check=True)
                mm.then_inc(down_done, 1)

            def slot(i, s):
                c, first = Chunk(i, s), s % 2 == 1
                embed(Group(i, s + 2))
                if s == -2:
                    turn_x(1, range(KF // 2))
                    pe.wait_ge(wt_evac, 6)
                    pe.wait_ge(qkv_w_centred, KE)
                if s == -1:
                    turn_x(1, range(KF // 2, KF))
                if 0 <= s < 3:
                    turn_ffn_weights(range(s * FW_SETS // FW_BATCH, (s + 1) * FW_SETS // FW_BATCH))
                if not first:
                    down(c, 1)
                    down(c, 2)
                    gate_up(c, 3)
                turn_probs(Group(i, s - 1))
                turn_xn2(Group(i, s - 2))
                scores(Group(i, s))
                if first:
                    gate_up(c, 0)
                else:
                    down(c, 3)
                    gate_up(c, 4)
                turn_xn1(Group(i, s + 2))
                attend(Group(i, s - 1))
                if not first:
                    gate_up(c, 5)
                turn_qk(Group(i, s + 1))
                project_qkv(Group(i, s + 2))
                if first:
                    gate_up(c, 1)
                    down(c, 0)
                else:
                    down(c, 4)
                    down(c, 5)
                project_out(Group(i, s - 1))
                if first:
                    gate_up(c, 2)

            def turn_ffn_weights(batches):
                pe.wait_ge(ident16_ready, 1)
                pe.wait_ge(w16_ready, 3)
                for b in batches:
                    if b == 0:
                        pe.wait_ge(xt_evac_act, (XTILES - 1) * XT_BATCHES + XT_BATCHES // 2)
                    if b >= 2:
                        pe.wait_ge(fwt_evac, b - 1)
                    for q in range(FW_BATCH):
                        w, n = divmod(b * FW_BATCH + q, FW_SETS)
                        src = w16[:, w, n * P:(n + 1) * P]
                        mm = pe.transpose(spare_ps[:, b % 2].bitcast(F16)[:, q * P:(q + 1) * P], src, ident16[:])
                    mm.then_inc(fwt_done, 1)

            slots(pe, slot)

        @block.scalar
        def _(act):
            def evac_x(batches):
                for n in batches:
                    act.wait_ge(xt_done, n + 1)
                    nc.scalar.copy(x_patches(n), x_turned(n)).then_inc(xt_evac_act, 1)

            def load_xs(g):
                if not g.real:
                    return
                if positive(g.n - 1):
                    act.wait_ge(emb_done, g.n - 1)
                act.dma_start(xs[:, g.buf], xpt.rearrange("p k b t -> p k (b t)")[:, :, bass.ds(g.n * GT, GT)]).then_inc(xs_loaded[g.buf], 16)

            evac_x(range(0, XT_BATCHES, 2))
            act.wait_ge(xt_evac_act, XT_BATCHES // 2)
            act.wait_ge(xt_evac_dve, XT_BATCHES // 2)
            act.wait_ge(xpt_zeroed, 1)
            load_xs(Group(0, 0))
            for m in range(4):
                act.wait_ge(wt_done, m + 1)
                nc.scalar.copy(wqkv[:, m // 2, (m % 2) * 3 * P:(m % 2 + 1) * 3 * P], (ptq_ps0, ptq_ps1)[m % 2][:, 0:3 * P]).then_inc(wt_evac, 1)
            for m in range(4, 6):
                act.wait_ge(wt_done, m + 1)
                nc.scalar.copy(wo[:, m - 4], (ptq_ps0, ptq_ps1)[m % 2][:, 0:EMB]).then_inc(wt_evac, 1)
            def evac_pt(g):
                if not g.real:
                    return
                if positive(g.n):
                    act.wait_ge(v2_free, g.n + 2)
                for b in range(2):
                    act.wait_ge(pt_done, 2 * g.n + b + 1)
                    nc.scalar.copy(pt[:, b * 4:(b + 1) * 4], (ptq_ps0, ptq_ps1)[b][0:PAIR, 0:4 * GT].rearrange("p (c t) -> p c t", c=4)).then_inc(pt_evac, 1)

            def exponentials(g):
                if not g.real:
                    return
                act.wait_ge(sub_done, g.n + 1)
                view = prob[0:GT, g.buf].rearrange("p j h k -> p (j h k)")
                nc.scalar.activation(view, view, ACT.Exp, scale=float(HD) ** -0.5).then_inc(exp_done, 1)

            def evac_ot(g):
                if not g.real:
                    return
                if positive(g.n):
                    act.wait_ge(o_done, g.n)
                act.wait_ge(v2_free, g.n + 3)
                nc.scalar.copy(ot[:], out_ps[:, 0:KE * GT].rearrange("p (k t) -> p k t", k=KE)).then_inc(ot_evac, 1)

            def evac_x1t(g):
                if not g.real:
                    return
                act.wait_ge(x1t_done, g.n + 1)
                nc.scalar.copy(x1t[:, g.buf], emb_ps[:, 0:KE * GT].rearrange("p (k t) -> p k t", k=KE)).then_inc(x1t_evac, 1)

            def evac_qkt(g):
                if not g.real:
                    return
                act.wait_ge(qkt_done, g.n + 1)
                for a in range(KE):
                    cp = nc.scalar.activation(qm[:, a].rearrange("p (i c) -> p i c", i=GI)[:, :, 0:TOK],
                                              emb_ps[:, a * GT:(a + 1) * GT].rearrange("p (i t) -> p i t", i=GI),
                                              ACT.Identity, bias=lnp[:, 1:2], scale=lnp[:, 0:1])
                cp.then_inc(qkt_evac, 1)
                for p in range(HR):
                    nc.scalar.activation(k2[:, :, p], emb_ps[:, KE * GT:2 * KE * GT].rearrange("p (a t) -> p a t", a=KE),
                                         ACT.Identity, bias=klnb[:, p:p + 1], scale=klnw[:, p:p + 1]).then_inc(qkt_evac, 1)

            def squares(g):
                if not g.real:
                    return
                act.wait_ge(qk_ready, g.n + 1)
                if positive(g.n):
                    act.wait_ge(ss_done, g.n)
                nc.scalar.activation(sq[0:GT], qk[0:GT, g.buf], ACT.Square).then_inc(sq_done, 1)

            def high_x2(g):
                if not g.real:
                    return
                act.wait_ge(x2t_done, g.n + 1)
                nc.scalar.copy(x2hi[:, :, bass.ds(g.n * GT, GT)], out_ps[:, 0:KE * GT].rearrange("p (k t) -> p k t", k=KE)).then_inc(x2hi_done, 1)

            def tanh_gate(c, m):
                if not c.real:
                    return
                T = c.groups * GT
                act.wait_ge(gu_done, c.n * MT + m + 1)
                nc.scalar.activation(th[:, m % 2, 0:T], gu_ps[:, 0:T], ACT.Tanh, scale=0.5 * QUANT / XSCALE).then_inc(tanh_done, 1)

            def high_hidden(c, m):
                if not c.real:
                    return
                T = c.groups * GT
                act.wait_ge(gu_free, c.n * MT + m + 2)
                nc.scalar.copy(hhi[:, m % 2, 0:T], hf[:, m % 2, 0:T]).then_inc(hhi_done, 1)

            def slot(i, s):
                c, first = Chunk(i, s), s % 2 == 1
                if s == 1:
                    act.wait_ge(xt_evac_act, XTILES * XT_BATCHES - XT_BATCHES // 2)
                load_xs(Group(i, s + 3))
                if s in (-2, -1):
                    first_batch = XT_BATCHES + (s + AHEAD) * XT_BATCHES // 2
                    evac_x(range(first_batch, first_batch + XT_BATCHES // 2))
                if s == -1:
                    act.wait_ge(ffn_loaded[1], 16)
                    nc.scalar.copy(w16[:, 1], wraw[:, 1]).then_inc(w16_ready, 1)
                    act.wait_ge(kln_ready, 1)
                    act.wait_ge(qm_zeroed, 1)
                if 0 <= s < 3:
                    evac_ffn_weights(range(s * FW_SETS // FW_BATCH, (s + 1) * FW_SETS // FW_BATCH))
                if not first:
                    tanh_gate(c, 3)
                evac_pt(Group(i, s - 1))
                high_x2(Group(i, s - 2))
                if not first:
                    high_hidden(c, 3)
                evac_x1t(Group(i, s + 2))
                tanh_gate(c, 0 if first else 4)
                exponentials(Group(i, s))
                high_hidden(c, 0 if first else 4)
                evac_ot(Group(i, s - 1))
                if not first:
                    tanh_gate(c, 5)
                evac_qkt(Group(i, s + 1))
                if not first:
                    high_hidden(c, 5)
                squares(Group(i, s + 2))
                if first:
                    tanh_gate(c, 1)
                    high_hidden(c, 1)
                    tanh_gate(c, 2)
                    high_hidden(c, 2)

            def evac_ffn_weights(batches):
                last = 3 * FW_SETS // FW_BATCH - 1
                for b in batches:
                    done = {last - 1: acc_free, last: gu_free}.get(b, fwt_evac)
                    act.wait_ge(fwt_done, b + 1)
                    w, n = divmod(b * FW_BATCH, FW_SETS)
                    src = spare_ps[:, b % 2].bitcast(F16)[:, 0:FW_BATCH * P]
                    if w < 2:
                        dst = (wgt, wut)[w].rearrange("p k (m c) -> p m k c", c=P)[:, n // KE:(n + FW_BATCH) // KE]
                        nc.scalar.copy(dst, src.rearrange("p (m k c) -> p m k c", k=KE, c=P)).then_inc(done, 1)
                    else:
                        for q in range(FW_BATCH):
                            k, m = divmod(n + q, MT)
                            cp = nc.scalar.copy(wdt[:, m, k * P:(k + 1) * P], src[:, q * P:(q + 1) * P])
                        cp.then_inc(done, 1)

            slots(act, slot)
            act.wait_ge(xs_loaded[NG % 2], 16 * (NG // 2 + 1))

        @block.vector
        def _(dve):
            dve.wait_ge(ident_ready, 1)
            nc.vector.tensor_copy(ident16[:], ident[:]).then_inc(ident16_ready, 1)
            for p in range(HR):
                cols = ident.rearrange("p (j q d) -> p j q d", q=HR, d=HD)[:, :, p]
                nc.vector.tensor_reduce(par[:, p:p + 1], cols, AX.XY, ALU.add).then_inc(par_ready, 1)

            def cut_x(t, features):
                for f in features:
                    dve.wait_ge(x_loaded[t][f // 2], 16)
                    if t > 0:
                        dve.wait_ge(xt_done, XT_BATCHES * (t - 1) + 2 * (f + 1))
                    nc.vector.tensor_copy(xcut[0:XROWS, f // 2, f % 2].rearrange("p w (a b) -> p a w b", b=PATCH),
                                          xrow[0:XROWS, t, f // 2, (f % 2) * HALF:(f % 2 + 1) * HALF]).then_inc(xcut_ready[t], 1)

            cut_x(0, range(KF))
            for n in range(1, XT_BATCHES, 2):
                dve.wait_ge(xt_done, n + 1)
                nc.vector.tensor_copy(x_patches(n), x_turned(n)).then_inc(xt_evac_dve, 1)
            dve.wait_ge(tok_turned, 1)
            nc.vector.tensor_copy(tok_add[0:GT], out_ps[0:GT, 0:EMB]).then_inc(tok_added, 1)
            dve.wait_ge(wt_evac, 4)
            for k in range(KE):
                nc.vector.tensor_reduce(wmean[:, k], wqkv[:, k, 0:2 * EMB].rearrange("p (h d) -> p h d", d=HD), AX.X, ALU.add).then_inc(means_done, 1)
            for k in range(KE):
                view = wqkv[:, k, 0:2 * EMB].rearrange("p (h d) -> p h d", d=HD)
                dve.wait_ge(means_done, KE + k)
                nc.vector.tensor_scalar(wmean[:, k], wmean[:, k], 1.0 / HD, None, ALU.mult).then_inc(means_done, 1)
                dve.wait_ge(means_done, KE + k + 1)
                nc.vector.tensor_tensor(view, view, wmean[:, k].unsqueeze(2).to_broadcast([P, 2 * HEADS, HD]), ALU.subtract).then_inc(qkv_w_centred, 1)
            dve.wait_ge(tok_added, 1)
            cut_x(1, range(KF // 2))

            def centre_bias():
                dve.wait_ge(rows_loaded, 16 * 2)
                bview = bqkv[0:GT, 0:2 * EMB].rearrange("p (h d) -> p h d", d=HD)
                nc.vector.tensor_reduce(bmean[0:GT], bview, AX.X, ALU.add).then_inc(bmeans_done, 1)
                dve.wait_ge(cols_loaded, 16 * 4)
                dve.wait_ge(par_ready, HR)
                nc.vector.tensor_scalar(klnw[:], par[:], lnp[:, 2:3], None, ALU.mult)
                nc.vector.tensor_scalar(klnb[:], par[:], lnp[:, 3:4], None, ALU.mult).then_inc(kln_ready, 1)
                dve.wait_ge(bmeans_done, 1)
                nc.vector.tensor_scalar(bmean[0:GT], bmean[0:GT], 1.0 / HD, None, ALU.mult).then_inc(bmeans_done, 1)
                dve.wait_ge(bmeans_done, 2)
                nc.vector.tensor_tensor(bview, bview, bmean[0:GT].unsqueeze(2).to_broadcast([GT, 2 * HEADS, HD]), ALU.subtract).then_inc(qkv_w_centred, 1)
                dve.wait_ge(qkv_w_centred, KE + 1)

            def shift_scores(g):
                if not g.real:
                    return
                view = score_ps[0:GT, :, 0:KE * HR * TOK].rearrange("p j (h k) -> p j h k", k=TOK)
                dve.wait_ge(scores_done, g.n + 1)
                nc.vector.tensor_reduce(smax[0:GT, g.buf].rearrange("p (j h) -> p j h", j=HG), view, AX.X, ALU.max).then_inc(max_done, 1)
                dve.wait_ge(max_done, g.n + 1)
                if positive(g.n - 1):
                    dve.wait_ge(pt_done, 2 * (g.n - 1))
                nc.vector.tensor_tensor(prob[0:GT, g.buf], view,
                                        smax[0:GT, g.buf].rearrange("p (j h) -> p j h", j=HG).unsqueeze(3).to_broadcast([GT, HG, KE * HR, TOK]),
                                        ALU.subtract).then_inc(sub_done, 1)

            def embed_tokens(g):
                if not g.real:
                    return
                dve.wait_ge(emb_done, g.n + 1)
                if positive(g.n - 1):
                    dve.wait_ge(res_ready, g.n - 1)
                nc.vector.tensor_tensor(h_emb[0:GT, g.buf], emb_ps[0:GT, 0:EMB], tok_add[0:GT], ALU.add).then_inc(h_ready, 1)
                dve.wait_ge(h_ready, g.n + 1)
                nc.vector.bn_stats(stats1[0:GT, g.buf], h_emb[0:GT, g.buf]).then_inc(stats1_done, 1)

            def token_variance(g):
                if not g.real:
                    return
                nc.vector.bn_aggr(mv1[0:GT, g.buf], stats1[0:GT, g.buf]).then_inc(mv1_done, 1)
                dve.wait_ge(mv1_done, g.n + 1)
                nc.vector.tensor_scalar(ve1[0:GT, g.buf:g.buf + 1], mv1[0:GT, g.buf, 1:2], LN_EPS, None, ALU.add).then_inc(ve1_done, 1)

            def sum_probs(g):
                if not g.real:
                    return
                dve.wait_ge(exp_done, g.n + 1)
                nc.vector.tensor_reduce(ssum[0:GT, g.buf], prob[0:GT, g.buf].rearrange("p j h k -> p (j h) k"), AX.X, ALU.add).then_inc(sum_done, 1)
                dve.wait_ge(sum_done, g.n + 1)
                nc.vector.reciprocal(rsum[0:GT, g.buf], ssum[0:GT, g.buf]).then_inc(rsum_done, 1)

            def norm_tokens(g):
                if not g.real:
                    return
                dve.wait_ge(rstd1_done, g.n + 1)
                if positive(g.n - 1):
                    dve.wait_ge(x1t_done, g.n - 1)
                nc.vector.tensor_scalar(xn1[0:GT, g.buf], h_emb[0:GT, g.buf], mv1[0:GT, g.buf, 0:1], rstd1[0:GT, g.buf:g.buf + 1],
                                        ALU.subtract, ALU.mult).then_inc(xn1_done, 1)

            def add_attention(g):
                if not g.real:
                    return
                dve.wait_ge(o_done, g.n + 1)
                dve.wait_ge(res_ready, g.n + 1)
                if positive(g.n):
                    dve.wait_ge(h2_kept, g.n)
                nc.vector.tensor_tensor(hcur[0:GT], out_ps[0:GT, 0:EMB], h2[0:GT, g.n], ALU.add).then_inc(h2_ready, 1)
                dve.wait_ge(h2_ready, g.n + 1)
                nc.vector.bn_stats(stats2[0:GT], hcur[0:GT]).then_inc(stats2_done, 1)

            def residual_variance(g):
                if not g.real:
                    return
                nc.vector.bn_aggr(mv2[0:GT], stats2[0:GT]).then_inc(mv2_done, 1)
                dve.wait_ge(mv2_done, g.n + 1)
                nc.vector.tensor_scalar(ve2[0:GT], mv2[0:GT, 1:2], LN_EPS, XSCALE ** -2, ALU.add, ALU.mult).then_inc(ve2_done, 1)

            def norm_residual(g):
                if not g.real:
                    return
                dve.wait_ge(rstd2_done, g.n + 1)
                nc.vector.tensor_scalar(xn2[0:GT], hcur[0:GT], mv2[0:GT, 0:1], rstd2[0:GT], ALU.subtract, ALU.mult).then_inc(xn2_done, 1)

            def bias_qkv(g):
                if not g.real:
                    return
                dve.wait_ge(qkv_done, g.n + 1)
                if positive(g.n - 1):
                    dve.wait_ge(qkt_done, g.n - 1)
                nc.vector.tensor_tensor(qk[0:GT, g.buf], ptq_ps0[0:GT], bqkv[0:GT, 0:2 * EMB], ALU.add).then_inc(qk_ready, 1)
                if positive(g.turn):
                    dve.wait_ge(v_moved[g.buf], 16 * 2 * GI * g.turn)
                nc.vector.tensor_tensor(vt[0:GT, g.buf].rearrange("p q d c -> p q c d"), ptq_ps1[0:GT, 0:EMB].rearrange("p (c q d) -> p q c d", q=2, d=HD),
                                        bqkv[0:GT, 2 * EMB:QKV].rearrange("p (c q d) -> p q c d", q=2, d=HD), ALU.add).then_inc(v_ready, 1)

            def sum_squares(g):
                if not g.real:
                    return
                dve.wait_ge(sq_done, g.n + 1)
                nc.vector.tensor_reduce(ss[0:GT, g.buf], sq[0:GT].rearrange("p (h d) -> p h d", d=HD), AX.X, ALU.add).then_inc(ss_done, 1)

            def variance_qk(g):
                if not g.real:
                    return
                dve.wait_ge(ss_done, g.n + 1)
                nc.vector.tensor_scalar(ve_qk[0:GT], ss[0:GT, g.buf], 1.0 / HD, LN_EPS, ALU.mult, ALU.add).then_inc(ve_qk_done, 1)

            def guess_rstd(g):
                if not g.real:
                    return
                y, half = rstd_qk[0:GT, g.buf], newton[0:GT]
                dve.wait_ge(ve_qk_done, g.n + 1)
                if positive(g.n - 1):
                    dve.wait_ge(qkn_done, g.n - 1)
                nc.vector.tensor_scalar(half.bitcast(I32), ve_qk[0:GT].bitcast(I32), 1, None, ALU.arith_shift_right).then_inc(newton_done, 1)
                dve.wait_ge(newton_done, g.n * NEWTON_OPS + 1)
                nc.vector.tensor_scalar(y.bitcast(I32), half.bitcast(I32), -1.0, RSQRT_MAGIC, ALU.mult, ALU.add).then_inc(newton_done, 1)

            def newton_turn(g, t):
                if not g.real:
                    return
                y, half = rstd_qk[0:GT, g.buf], newton[0:GT]
                count = g.n * NEWTON_OPS + 3 * t + 2
                dve.wait_ge(newton_done, count)
                nc.vector.scalar_tensor_tensor(out=half, in0=y, scalar=-0.5, in1=y, op0=ALU.mult, op1=ALU.mult).then_inc(newton_done, 1)
                dve.wait_ge(newton_done, count + 1)
                nc.vector.tensor_tensor(half, half, ve_qk[0:GT], ALU.mult).then_inc(newton_done, 1)
                dve.wait_ge(newton_done, count + 2)
                nc.vector.scalar_tensor_tensor(out=y, in0=half, scalar=1.5, in1=y, op0=ALU.add, op1=ALU.mult)\
                    .then_inc(newton_done if t < NEWTON_TURNS - 1 else rstd_qk_done, 1)

            def low_x2(g):
                if not g.real:
                    return
                dve.wait_ge(x2hi_done, g.n + 1)
                nc.vector.tensor_tensor(x2lo[:, :, bass.ds(g.n * GT, GT)], out_ps[:, 0:KE * GT].rearrange("p (k t) -> p k t", k=KE),
                                        x2hi[:, :, bass.ds(g.n * GT, GT)], ALU.subtract).then_inc(x2lo_done, 1)

            def hidden(c, m):
                if not c.real:
                    return
                n, T = c.n * MT + m, c.groups * GT
                dve.wait_ge(tanh_done, n + 1)
                nc.vector.scalar_tensor_tensor(out=gated[:, m % 2, 0:T], in0=th[:, m % 2, 0:T], scalar=1.0, in1=gu_ps[:, 0:T],
                                               op0=ALU.add, op1=ALU.mult).then_inc(gated_done, 1)
                dve.wait_ge(gated_done, n + 1)
                nc.vector.scalar_tensor_tensor(out=hf[:, m % 2, 0:T], in0=gu_ps[:, T:2 * T], scalar=0.5 * (QUANT / XSCALE) ** 2 * HSCALE,
                                               in1=gated[:, m % 2, 0:T], op0=ALU.mult, op1=ALU.mult).then_inc(gu_free, 1)

            def add_ffn(c):
                if not c.real:
                    return
                dve.wait_ge(down_done, (c.n + 1) * MT)
                dve.wait_ge(h2_kept, c.n * CG + c.groups)
                for q in range(c.groups):
                    row = h2[0:GT, c.n * CG + q]
                    y = nc.vector.scalar_tensor_tensor(out=row, in0=acc_ps[0:GT, q * EMB:(q + 1) * EMB], scalar=QUANT / HSCALE,
                                                       in1=row, op0=ALU.mult, op1=ALU.add)
                y.then_inc(acc_free, 1)

            def slot(i, s):
                embedded, attended = Group(i, s + 2), Group(i, s - 1)
                c, first = Chunk(i, s), s % 2 == 1
                embed_tokens(embedded)
                if embedded.real:
                    dve.wait_ge(stats1_done, embedded.n + 1)
                newton_turn(Group(i, s + 1), 1)
                token_variance(embedded)
                newton_turn(Group(i, s + 1), 2)
                norm_tokens(embedded)
                if not first:
                    hidden(c, 3)
                low_x2(Group(i, s - 2))
                shift_scores(Group(i, s))
                hidden(c, 0 if first else 4)
                sum_probs(Group(i, s))
                if not first:
                    hidden(c, 5)
                if s == -2:
                    centre_bias()
                    cut_x(1, range(KF // 2, KF))
                if s == -1:
                    for w in (0, 2):
                        dve.wait_ge(ffn_loaded[w], 16)
                        nc.vector.tensor_copy(w16[:, w], wraw[:, w]).then_inc(w16_ready, 1)
                bias_qkv(embedded)
                if first:
                    hidden(c, 1)
                add_attention(attended)
                if attended.real:
                    dve.wait_ge(stats2_done, attended.n + 1)
                sum_squares(embedded)
                residual_variance(attended)
                if first:
                    hidden(c, 2)
                variance_qk(embedded)
                guess_rstd(embedded)
                norm_residual(attended)
                newton_turn(embedded, 0)
                if not first:
                    add_ffn(c)

            slots(dve, slot)


_INS = ["x", "cls_tok", "L0_tok_W", "L0_tok_b", "L0_tok_cls_token", "L0_tok_pos_emb", "L0_attn_qkv_w", "L0_attn_qkv_b",
        "L0_attn_o_w", "L0_attn_o_b", "L0_attn_q_norm_w", "L0_attn_q_norm_b", "L0_attn_k_norm_w", "L0_attn_k_norm_b",
        "L0_ffn_w_gate", "L0_ffn_w_up", "L0_ffn_w_down"]


def kernel(**inputs):
    import numpy as _np
    import concourse.bacc as _bacc
    from concourse.bass_utils import run_bass_kernel_spmd as _run

    nc = _bacc.Bacc("TRN2", target_bir_lowering=False, num_devices=1)
    arrays, args = {}, []
    for name in _INS:
        a = _np.ascontiguousarray(inputs[name])
        arrays[f"in_{name}"] = a
        args.append(nc.dram_tensor(f"in_{name}", a.shape, mybir.dt.from_np(a.dtype), kind="ExternalInput").ap())
    args.append(nc.dram_tensor("out_0", (IMAGES, TOK, EMB), F32, kind="ExternalOutput").ap())
    vit_kernel(nc, *args)
    r = _run(nc, [arrays], core_ids=[0])
    return r.results[0]["out_0"]
```

```python
from contextlib import ExitStack

import concourse.bass as bass
from concourse import mybir
from concourse.alu_op_type import AluOpType as ALU

ACT = mybir.ActivationFunctionType
F32 = mybir.dt.float32
F16 = mybir.dt.float16
I32 = mybir.dt.int32
AX = mybir.AxisListType

P = 128
BANK = 512

IMAGES, CH, SIDE, PATCH = 32, 3, 96, 16
GRID = SIDE // PATCH
EMB = 256
KE = EMB // P
TOK = GRID * GRID + 2
TABLE = TOK + 2
FEAT = CH * PATCH * PATCH
KF = FEAT // P
HALF = PATCH // 2

GI = 3
GT = GI * TOK
NG = -(-IMAGES // GI)
LAST_ROWS = (IMAGES - GI * (NG - 1)) * TOK
XIMG = 16
XROWS = XIMG * GRID
XTILES = IMAGES // XIMG

HEADS, HD = 16, 16
QKV = 3 * EMB
SIDE_HEADS = P // TOK
CH_HEADS = P // HD
BLOCKS = GI * KE * SIDE_HEADS
SB = 2
PAIR = 2 * TOK
NPAIR = HEADS // 2
PT_IM = NPAIR * TOK
HID = 768
MT = HID // P
RING = 3
TAIL_RING = 4
CG = 2
NCH = -(-NG // CG)
LN_EPS = 1e-5
RSQRT_MAGIC = float(0x5F3759DF)
NEWTON_TURNS = 3
FFN_SLOT = 3
NEWTON_OPS = 3 * NEWTON_TURNS + 1
QUANT = 1.0 / 127.0
XSCALE = 2.0 ** 11
HSCALE = 2.0 ** -3


class Group:

    def __init__(self, i, c):
        self.n = 2 * i + c
        self.buf = c % 2
        self.turn = i + c // 2
        self.real = not isinstance(self.n, int) or 0 <= self.n < NG


class Chunk:

    def __init__(self, i, s):
        self.n = i + (s - FFN_SLOT) // 2
        known = isinstance(self.n, int)
        self.real = not known or 0 <= self.n < NCH
        self.groups = min(CG, NG - CG * self.n) if known else CG
        self.folds = CG // self.groups
        self.tiles = MT // self.folds


def positive(n):
    return not isinstance(n, int) or n > 0


def vit_kernel(nc, x, cls_tok, w_emb, b_emb, cls_token, pos_emb, qkv_w, qkv_b, o_w, o_b,
               qn_w, qn_b, kn_w, kn_b, w_gate, w_up, w_down, out):
    with ExitStack() as ctx:
        def sb(name, shape, dt=F32):
            return ctx.enter_context(nc.sbuf_tensor(name, shape, dt))

        def sem(name):
            return ctx.enter_context(nc.semaphore(name))

        ident = sb("ident", [P, P])
        ident16 = sb("ident16", [P, P], F16)
        xrow = sb("xrow", [P, XTILES, CH, PATCH, GRID, PATCH])
        xcut = sb("xcut", [P, CH, 2, GRID, HALF * PATCH])
        xpt = sb("xpt", [P, KF, (NG + 1) * GI, TOK])
        xs = sb("xs", [P, 2, KF, GT])
        wemb = sb("wemb", [P, CH, 2, EMB])
        wqkv_raw = sb("wqkv_raw", [P, QKV // P, EMB])
        wqkv = sb("wqkv", [P, KE, QKV])
        wo_raw = sb("wo_raw", [P, KE, EMB])
        wo = sb("wo", [P, KE, EMB])
        wmean = sb("wmean", [P, KE, 2 * HEADS])
        bqkv = sb("bqkv", [P, QKV])
        bmean = sb("bmean", [P, 2 * HEADS])
        bo = sb("bo", [P, EMB])
        row_table = sb("row_table", [TABLE, EMB])
        row_sel = sb("row_sel", [TABLE, GT])
        tok_add = sb("tok_add", [P, EMB])
        lnp = sb("lnp", [P, 4])
        par = sb("par", [P, SIDE_HEADS ** 2])
        qln = sb("qln", [P, 3, SIDE_HEADS])
        kln = sb("kln", [P, 3, SIDE_HEADS])
        bv = sb("bv", [P, EMB])
        mhalf = sb("mhalf", [P, 1])

        h_emb = sb("h_emb", [P, 2, EMB])
        stats1 = sb("stats1", [P, 2, 6])
        mv1 = sb("mv1", [P, 2, 2])
        ve1 = sb("ve1", [P, 2])
        rstd1 = sb("rstd1", [P, 2])
        xn1 = sb("xn1", [P, 2, EMB])
        x1t = sb("x1t", [P, 2, KE, GT])
        qk = sb("qk", [P, 2, 2 * EMB])
        sq = sb("sq", [P, 2 * EMB])
        ss = sb("ss", [P, 2, 2 * HEADS])
        ve_qk = sb("ve_qk", [P, 2 * HEADS])
        rstd_qk = sb("rstd_qk", [P, 2, 2 * HEADS])
        newton = sb("newton", [P, 2 * HEADS])
        vt = sb("vt", [P, 2, 2, HD, HEADS // 2])
        v2 = sb("v2", [PAIR, 2, GI, 2 * HD, HEADS // 2])
        qh = sb("qh", [P, KE, GI, SIDE_HEADS, TOK])
        kh = sb("kh", [P, KE * SIDE_HEADS, GT])
        prob = sb("prob", [P, 2, BLOCKS, TOK])
        smax = sb("smax", [P, 2, BLOCKS])
        ssum = sb("ssum", [P, 2, BLOCKS])
        rsum = sb("rsum", [P, 2, BLOCKS])
        ot = sb("ot", [P, KE, GT])
        h2 = sb("h2", [P, NG, EMB])
        hcur = sb("hcur", [P, EMB])
        stats2 = sb("stats2", [P, 6])
        mv2 = sb("mv2", [P, 2])
        ve2 = sb("ve2", [P, 1])
        rstd2 = sb("rstd2", [P, 1])
        xn2 = sb("xn2", [P, EMB])
        x2hi = sb("x2hi", [P, KE, NG * GT], F16)
        x2lo = sb("x2lo", [P, KE, NG * GT], F16)

        pt = xrow.rearrange("p t c a w b -> p t (c a w b)")[0:PAIR, 1, 0:GI * PT_IM]
        wo_pairs = prob[:, 1].rearrange("p b k -> p (b k)")[:, 0:KE * EMB].rearrange("p (t e) -> p t e", t=KE)

        wraw = xrow.rearrange("p t c a w b -> p t (c a w b)")[:, 0].bitcast(I32).rearrange("p (n e) -> p n e", n=3)
        w16 = sb("w16", [P, 3, MT * EMB], F16)
        wgt = sb("wgt", [P, KE, HID], F16)
        wut = sb("wut", [P, KE, HID], F16)
        wdt = sb("wdt", [P, MT, EMB], F16)
        th = sb("th", [P, TAIL_RING, CG * GT])
        hf = wqkv_raw.rearrange("p t k -> p (t k)")[:, 0:TAIL_RING * CG * GT].rearrange("p (r t) -> p r t", r=TAIL_RING)
        hhi = sb("hhi", [P, TAIL_RING, CG * GT], F16)
        hlo = sb("hlo", [P, TAIL_RING, CG * GT], F16)

        def bank(name):
            return ctx.enter_context(nc.psum_tensor(name, [P, BANK], F32))

        score_ps = ctx.enter_context(nc.psum_tensor("score_ps", [P, SB, BANK], F32))
        spare_ps = ctx.enter_context(nc.psum_tensor("spare_ps", [P, 2, BANK], F32))
        gu_ps, acc_ps = spare_ps[:, 0], spare_ps[:, 1]
        ptq_ps0, ptq_ps1, out_ps, emb_ps = bank("ptq_ps0"), bank("ptq_ps1"), bank("out_ps"), bank("emb_ps")
        x_banks = [score_ps[:, 0], score_ps[:, 1], spare_ps[:, 0], spare_ps[:, 1]]

        x_loaded = [[sem(f"x_loaded{t}_{c}") for c in range(CH)] for t in range(XTILES)]
        wemb_loaded, wqkv_loaded, wo_loaded = sem("wemb_loaded"), sem("wqkv_loaded"), sem("wo_loaded")
        ffn_loaded = [sem(f"ffn_loaded{i}") for i in range(3)]
        rows_loaded, cols_loaded = sem("rows_loaded"), sem("cols_loaded")
        ident_zero, ident_ready, ident16_ready = sem("ident_zero"), sem("ident_ready"), sem("ident16_ready")
        table_loaded, sel_zero, sel_ready, tok_turned = sem("table_loaded"), sem("sel_zero"), sem("sel_ready"), sem("tok_turned")
        xpt_zeroed = sem("xpt_zeroed")
        mhalf_ready = sem("mhalf_ready")
        par_ready, tok_added, qkv_w_centred = sem("par_ready"), sem("tok_added"), sem("qkv_w_centred")
        means_done, bmeans_done, qln_ready = sem("means_done"), sem("bmeans_done"), sem("qln_ready")
        bv_ready = sem("bv_ready")
        wo_ordered = sem("wo_ordered")
        xcut_pool_ready, xcut_last_ready = sem("xcut_pool_ready"), sem("xcut_last_ready")
        xcut_ready = [sem(f"xcut_ready{t}") for t in range(XTILES)]
        xt_done, xt_evac_act, xt_evac_dve = sem("xt_done"), sem("xt_evac_act"), sem("xt_evac_dve")
        wt_done, wt_evac = sem("wt_done"), sem("wt_evac")

        xs_loaded = [sem(f"xs_loaded{b}") for b in range(2)]
        v_moved = [sem(f"v_moved{b}") for b in range(2)]
        emb_done, x1t_done, qk_done, v_done = sem("emb_done"), sem("x1t_done"), sem("qk_done"), sem("v_done")
        qkt_done, scores_done, pt_done = sem("qkt_done"), sem("scores_done"), sem("pt_done")
        v2_free, o_done, x2t_done = sem("v2_free"), sem("o_done"), sem("x2t_done")
        h_ready, stats1_done, mv1_done, ve1_done = sem("h_ready"), sem("stats1_done"), sem("mv1_done"), sem("ve1_done")
        rstd1_done, xn1_done = sem("rstd1_done"), sem("xn1_done")
        res_ready, x1t_evac = sem("res_ready"), sem("x1t_evac")
        qk_ready, v_ready, sq_done, ss_done = sem("qk_ready"), sem("v_ready"), sem("sq_done"), sem("ss_done")
        newton_done = sem("newton_done")
        ve_qk_done, rstd_qk_done, qkn_done, qkt_evac = sem("ve_qk_done"), sem("rstd_qk_done"), sem("qkn_done"), sem("qkt_evac")
        max_done, sub_done, exp_done, sum_done = sem("max_done"), sem("sub_done"), sem("exp_done"), sem("sum_done")
        rsum_done, probs_ready, pt_evac, ot_evac = sem("rsum_done"), sem("probs_ready"), sem("pt_evac"), sem("ot_evac")
        h2_kept = sem("h2_kept")
        h2_ready, stats2_done, mv2_done, ve2_done = sem("h2_ready"), sem("stats2_done"), sem("mv2_done"), sem("ve2_done")
        rstd2_done, xn2_done, x2hi_done, x2lo_done = sem("rstd2_done"), sem("xn2_done"), sem("x2hi_done"), sem("x2lo_done")

        w16_ready, fwt_done, fwt_evac = sem("w16_ready"), sem("fwt_done"), sem("fwt_evac")
        gu_free, gu_done, tanh_done, gated_done = sem("gu_free"), sem("gu_done"), sem("tanh_done"), sem("gated_done")
        hhi_done, hlo_done, down_done = sem("hhi_done"), sem("hlo_done"), sem("down_done")
        acc_free, y_stored = sem("acc_free"), sem("y_stored")

        out_rows = out.rearrange("b t e -> (b t) e")
        FW_SETS = MT * KE
        FW_BATCH = 4
        QKT_EVACS = 2 * SIDE_HEADS
        PT_SPLIT = PT_IM + GT
        XCUT_FIRST = 2
        ACT_CUTS = 4
        XT_WP = 3
        XT_BATCHES = KF * (GRID // XT_WP)
        W_BATCHES = (QKV // P) * KE // 4 + KE * KE // 4

        AHEAD = 2
        LOOP_SLOT = FFN_SLOT + 2
        steady = (NG - AHEAD - LOOP_SLOT) // 2
        assert LOOP_SLOT + 2 * steady == NG - AHEAD and NCH * CG == NG + 1
        g0, g1, g2, g3 = (Group(0, n) for n in range(4))
        g7, g8, g9, g10 = (Group(0, NG - n) for n in (4, 3, 2, 1))
        c2, c3, c4, c5 = (Chunk(0, FFN_SLOT + 2 * (NCH - n)) for n in (4, 3, 2, 1))

        def tail_tile(c, m):
            return c.n * MT + m - (c3.n * MT + MT // 2) if isinstance(c.n, int) else -1

        def in_tail(c, m):
            return tail_tile(c, m) >= 0

        def ring(c, m):
            return tail_tile(c, m) % TAIL_RING if in_tail(c, m) else m % RING

        def gu_bank(c, m):
            return (emb_ps, gu_ps, score_ps[:, 1], ptq_ps0)[tail_tile(c, m) % TAIL_RING] if in_tail(c, m) else gu_ps

        def x2_bank(g):
            return {g7.n: emb_ps, g9.n: ptq_ps1, g10.n: ptq_ps1}.get(g.n, out_ps) if isinstance(g.n, int) else out_ps

        def acc_bank(c):
            return score_ps[:, 0] if in_tail(c, 0) and c.n == c5.n else acc_ps

        def x_bank(n):
            return x_banks[n % len(x_banks)]

        def dve_evacuates(n):
            return n % 2 == 1 if n < XT_BATCHES else XT_BATCHES // 3 <= n - XT_BATCHES < 2 * XT_BATCHES // 3

        def wait_x_evac(eng, n):
            count = sum(dve_evacuates(b) == dve_evacuates(n) for b in range(n + 1))
            eng.wait_ge(xt_evac_dve if dve_evacuates(n) else xt_evac_act, count)

        def wait_all_x(eng, load):
            for by_dve in (False, True):
                wait_x_evac(eng, max(n for n in range(load * XT_BATCHES, (load + 1) * XT_BATCHES) if dve_evacuates(n) == by_dve))

        def x_bank_free(eng, n):
            if n >= len(x_banks):
                wait_x_evac(eng, n - len(x_banks))

        FIRST_XS = LOOP_SLOT + AHEAD
        def embedded_from_xpt(g):
            return isinstance(g.n, int) and g.n < FIRST_XS

        def xs_turns(g):
            return g.turn - (FIRST_XS + (g.buf - FIRST_XS) % 2) // 2 + 1

        def ffn_batches(w):
            return range(w * FW_SETS // FW_BATCH, (w + 1) * FW_SETS // FW_BATCH)

        def slots(eng, run_slot):
            for s in range(LOOP_SLOT):
                run_slot(0, s)
            with eng.Fori(0, steady) as i:
                run_slot(i, LOOP_SLOT)
                run_slot(i, LOOP_SLOT + 1)

        def pair_order(dst, src):
            for a, at in ((0, 0), (1, EMB - 3 * 2 * HD)):
                yield (dst[:, at:at + 4 * HD].rearrange("p (i q d) -> p i q d", i=2, q=2),
                       src[:, a * P:a * P + 6 * HD].rearrange("p (i x d) -> p i x d", i=2, x=3)[:, :, 0:2])
                yield dst[:, at + 4 * HD:at + 6 * HD], src[:, a * P + 6 * HD:(a + 1) * P]
            yield (dst[:, 6 * HD:10 * HD].rearrange("p (i q d) -> p i q d", i=2, q=2),
                   src.rearrange("p (q h d) -> p h q d", q=2, d=HD)[:, 2:6:3])
        PIECES = 5

        def kh_slots(j):
            second = SIDE_HEADS + (j + 1) % SIDE_HEADS
            return slice(j, second + 1, second - j)

        def half_patches(t, f):
            return xrow[0:XROWS, t, f // 2, (f % 2) * HALF:(f % 2 + 1) * HALF]

        def xcut_at(f):
            return xcut[0:XROWS, f // 2, f % 2].rearrange("p w (a b) -> p a w b", b=PATCH)

        def emb_bank(g):
            return out_ps if isinstance(g.n, int) and g.n in (1, 2, 3) else emb_ps

        def x_turned(n):
            return x_bank(n)[:, 0:XT_WP * XROWS].rearrange("p (wp b hp) -> p wp b hp", wp=XT_WP, b=XIMG)

        def x_patches(n):
            t, f, w0 = n // XT_BATCHES, n % XT_BATCHES // (GRID // XT_WP), n % (GRID // XT_WP) * XT_WP
            tokens = xpt[:, f, t * XIMG:(t + 1) * XIMG, 2:TOK]
            return tokens.rearrange("p b (hp wp) -> p wp b hp", wp=GRID)[:, w0:w0 + XT_WP]

        block = ctx.enter_context(nc.Block())

        @block.sync
        def _(sp):
            x_dram = x.rearrange("b c (hp p1) w -> b hp c (p1 w)", p1=PATCH)
            xrow_flat = xrow.rearrange("p t c a w b -> p t c (a w b)")

            def load_x(t):
                for c in range(CH):
                    sp.dma_start(xrow_flat[0:XROWS, t, c], x_dram[t * XIMG:(t + 1) * XIMG, :, c]).then_inc(x_loaded[t][c], 16)

            sp.dma_start(wqkv_raw[:], qkv_w.rearrange("(t p) k -> p t k", p=P)).then_inc(wqkv_loaded, 16)
            load_x(0)
            w_dram = w_emb.rearrange("(h p c) e -> p h (c e)", h=2, p=P)
            for hh in range(2):
                sp.dma_start(wemb[:, :, hh, :], w_dram[:, hh].rearrange("p (c e) -> p c e", c=CH)).then_inc(wemb_loaded, 16)
            sp.dma_start(row_table[0:1], cls_tok.rearrange("a b e -> (a b) e")).then_inc(table_loaded, 16)
            sp.dma_start(row_table[1:TOK], pos_emb).then_inc(table_loaded, 16)
            sp.dma_start(row_table[TOK:TOK + 1], cls_token.rearrange("a b e -> (a b) e")).then_inc(table_loaded, 16)
            sp.dma_start(row_table[TOK + 1:TABLE], b_emb.rearrange("(a e) -> a e", a=1)).then_inc(table_loaded, 16)
            sp.dma_start(wo_raw[:], o_w.rearrange("(t p) k -> p t k", p=P)).then_inc(wo_loaded, 16)
            sp.dma_start(bqkv[0:GT], qkv_b.partition_broadcast(GT)).then_inc(rows_loaded, 16)
            sp.dma_start(bo[0:GT], o_b.partition_broadcast(GT)).then_inc(rows_loaded, 16)
            for n, v in enumerate((qn_w, qn_b, kn_w, kn_b)):
                sp.dma_start(lnp[:, n:n + 1], v.partition_broadcast(P // HD).rearrange("r (d a) -> r d a", a=1)).then_inc(cols_loaded, 16)
            load_x(1)
            sp.wait_ge(xcut_ready[0], KF - 1)
            sp.wait_ge(xcut_last_ready, 1)
            for n, w in enumerate((w_gate, w_up)):
                sp.dma_start(wraw[:, n].rearrange("p (t k) -> p t k", t=MT), w.rearrange("(t p) k -> p t k", p=P)).then_inc(ffn_loaded[n], 16)
            sp.dma_start(wraw[:, 2].rearrange("p (t k) -> p t k", t=KE), w_down.rearrange("(t p) k -> p t k", p=P)).then_inc(ffn_loaded[2], 16)

            def move_v(g):
                if not g.real:
                    return
                count = g.n + 1
                sp.wait_ge(v_ready, count)
                sp.wait_ge(v2_free, count)
                for im in range(GI):
                    for hp in range(2):
                        sp.dma_start(v2[hp * TOK:(hp + 1) * TOK, g.buf, im, hp * HD:(hp + 1) * HD], vt[im * TOK:(im + 1) * TOK, g.buf, hp]).then_inc(v_moved[g.buf], 16)


            def slot(i, s):
                move_v(Group(i, s + 1))

            move_v(g0)
            slots(sp, slot)
            move_v(g10)

            for c in range(NCH):
                sp.wait_ge(acc_free, c + 2)
                for g in range(c * CG, min((c + 1) * CG, NG)):
                    rows = GT if g < NG - 1 else LAST_ROWS
                    sp.dma_start(out_rows[g * GT:g * GT + rows], h2[0:rows, g]).then_inc(y_stored, 16)
            sp.wait_ge(y_stored, 16 * NG)

        @block.gpsimd
        def _(pool):
            nc.gpsimd.memset(ident[:], 0.0).then_inc(ident_zero, 1)
            pool.wait_ge(ident_zero, 1)
            nc.gpsimd.affine_select(out=ident[:], in_=ident[:], compare_op=ALU.not_equal, fill=1.0, base=0,
                                    pattern=[[-1, P]], channel_multiplier=1).then_inc(ident_ready, 1)
            nc.gpsimd.memset(row_sel[:], 0.0).then_inc(sel_zero, 1)
            images = [[0, GI], [1, TOK]]
            pool.wait_ge(sel_zero, 1)
            nc.gpsimd.affine_select(out=row_sel[:], in_=row_sel[:], compare_op=ALU.not_equal, fill=1.0, base=0,
                                    pattern=images, channel_multiplier=-1).then_inc(sel_zero, 1)
            pool.wait_ge(sel_zero, 2)
            nc.gpsimd.affine_select(out=row_sel[:], in_=row_sel[:], compare_op=ALU.not_equal, fill=1.0, base=-1 - P * TOK,
                                    pattern=images, channel_multiplier=P).then_inc(sel_zero, 1)
            pool.wait_ge(sel_zero, 3)
            nc.gpsimd.affine_select(out=row_sel[:], in_=row_sel[:], compare_op=ALU.is_gt, fill=1.0, base=2 + P * (TOK + 1),
                                    pattern=[[0, GI], [-1, TOK]], channel_multiplier=-P).then_inc(sel_ready, 1)
            nc.gpsimd.memset(xpt[:, :, IMAGES:(NG + 1) * GI, :], 0.0)
            nc.gpsimd.memset(xpt[:, :, 0:IMAGES, 0:2], 0.0).then_inc(xpt_zeroed, 1)
            nc.gpsimd.memset(mhalf[:], -0.5).then_inc(mhalf_ready, 1)
            for b in range(2):
                nc.gpsimd.memset(v2[:, b], 0.0).then_inc(v2_free, 1)

            pool.wait_ge(wo_loaded, 16)
            for t in range(KE):
                for dst, src in pair_order(wo_pairs[:, t], wo_raw[:, t]):
                    nc.gpsimd.tensor_copy(dst, src).then_inc(wo_ordered, 1)
            pool.wait_ge(rows_loaded, 16 * 2)
            pool.wait_ge(mhalf_ready, 1)

            def residual(g):
                if not g.real:
                    return
                pool.wait_ge(h_ready, g.n + 1)
                nc.gpsimd.tensor_tensor(h2[0:GT, g.n], h_emb[0:GT, g.buf], bo[0:GT], ALU.add).then_inc(res_ready, 1)

            def rstd_of_tokens(g):
                if not g.real:
                    return
                pool.wait_ge(ve1_done, g.n + 1)
                nc.gpsimd.tensor_tensor(rstd1[0:GT, g.buf:g.buf + 1], ve1[0:GT, g.buf:g.buf + 1],
                                        mhalf[0:GT], ALU.pow).then_inc(rstd1_done, 1)

            def rstd_of_residual(g):
                if not g.real:
                    return
                pool.wait_ge(ve2_done, g.n + 1)
                nc.gpsimd.tensor_tensor(rstd2[0:GT], ve2[0:GT], mhalf[0:GT], ALU.pow).then_inc(rstd2_done, 1)

            def keep_residual(g):
                if not g.real:
                    return
                pool.wait_ge(h2_ready, g.n + 1)
                nc.gpsimd.tensor_copy(h2[0:GT, g.n], hcur[0:GT]).then_inc(h2_kept, 1)

            def norm_qk(g):
                if not g.real:
                    return
                pool.wait_ge(rstd_qk_done, g.n + 1)
                view = qk[0:GT, g.buf].rearrange("p (h d) -> p h d", d=HD)
                nc.gpsimd.tensor_tensor(view, view, rstd_qk[0:GT, g.buf].unsqueeze(2).to_broadcast([GT, 2 * HEADS, HD]),
                                        ALU.mult).then_inc(qkn_done, 1)

            def squares(g):
                pool.wait_ge(qk_ready, g.n + 1)
                pool.wait_ge(ss_done, g.n)
                nc.gpsimd.tensor_tensor(sq[0:GT], qk[0:GT, g.buf], qk[0:GT, g.buf], ALU.mult).then_inc(sq_done, 1)

            def norm_probs(g):
                if not g.real:
                    return
                pool.wait_ge(rsum_done, g.n + 1)
                view = prob[0:GT, g.buf]
                nc.gpsimd.tensor_tensor(view, view, rsum[0:GT, g.buf].unsqueeze(2).to_broadcast([GT, BLOCKS, TOK]),
                                        ALU.mult).then_inc(probs_ready, 1)

            def low_hidden(c, m):
                if not c.real:
                    return
                n, T = c.n * MT + m, CG * GT
                pool.wait_ge(hhi_done, n + 1)
                nc.gpsimd.tensor_tensor(hlo[:, ring(c, m), 0:T], hf[:, ring(c, m), 0:T], hhi[:, ring(c, m), 0:T], ALU.subtract).then_inc(hlo_done, 1)

            def slot(i, s):
                c, first = Chunk(i, s), s % 2 == 1
                if s > 1:
                    rstd_of_tokens(Group(i, s + 2))
                    residual(Group(i, s + 2))
                if not first:
                    low_hidden(c, 3)
                norm_qk(Group(i, s + 1))
                if first:
                    low_hidden(c, 0)
                    norm_probs(Group(i, s))
                    low_hidden(c, 1)
                    rstd_of_residual(Group(i, s - 1))
                    keep_residual(Group(i, s - 1))
                    low_hidden(c, 2)
                else:
                    low_hidden(c, 4)
                    norm_probs(Group(i, s))
                    if s == 0:
                        rstd_of_tokens(g3)
                        residual(g3)
                    low_hidden(c, 5)
                    rstd_of_residual(Group(i, s - 1))
                    keep_residual(Group(i, s - 1))

            for g in (g0, g1):
                rstd_of_tokens(g)
                residual(g)
            for f in range(ACT_CUTS, KF):
                pool.wait_ge(x_loaded[1][f // 2], 16)
                pool.wait_ge(xt_done, 2 * (f + 1))
                nc.gpsimd.tensor_copy(xcut_at(f), half_patches(1, f)).then_inc(xcut_pool_ready, 1)
            norm_qk(g0)
            squares(g1)
            rstd_of_tokens(g2)
            residual(g2)
            slots(pool, slot)
            norm_qk(g10)
            low_hidden(c3, 0)
            low_hidden(c3, 1)
            norm_probs(g9)
            rstd_of_residual(g8)
            low_hidden(c3, 2)
            keep_residual(g8)
            low_hidden(c3, 3)
            norm_probs(g10)
            low_hidden(c3, 4)
            rstd_of_residual(g9)
            low_hidden(c3, 5)
            keep_residual(g9)
            rstd_of_residual(g10)
            low_hidden(c4, 0)
            low_hidden(c4, 1)
            keep_residual(g10)
            for m in range(2, MT):
                low_hidden(c4, m)
            for m in range(c5.tiles):
                low_hidden(c5, m)

        @block.tensor
        def _(pe):
            pe.wait_ge(ident_ready, 1)

            def turn_x(t, features=range(KF)):
                for f in features:
                    if t == 0 and f == KF - 1:
                        pe.wait_ge(xcut_last_ready, 1)
                    elif t == 0 or f < ACT_CUTS:
                        pe.wait_ge(xcut_ready[t], f + 1)
                    else:
                        pe.wait_ge(xcut_pool_ready, f + 1 - ACT_CUTS)
                    for w0 in range(0, GRID, XT_WP):
                        n = t * XT_BATCHES + f * (GRID // XT_WP) + w0 // XT_WP
                        x_bank_free(pe, n)
                        for w in range(XT_WP):
                            mm = pe.transpose(x_bank(n)[:, w * XROWS:(w + 1) * XROWS], xcut[0:XROWS, f // 2, f % 2, w0 + w],
                                              ident[0:XROWS, 0:XROWS])
                        mm.then_inc(xt_done, 1)

            def turn_weights(raw, tiles, step, m):
                for k in range(KE):
                    for r0 in range(0, tiles, step):
                        if m >= 2:
                            pe.wait_ge(wt_evac, m - 1)
                        for r in range(step):
                            mm = pe.transpose((ptq_ps0, ptq_ps1)[m % 2][:, r * P:(r + 1) * P], raw[:, r0 + r, k * P:(k + 1) * P], ident[:])
                        mm.then_inc(wt_done, 1)
                        m += 1

            pe.wait_ge(wqkv_loaded, 16)
            turn_weights(wqkv_raw, QKV // P, 3, 0)
            turn_x(0)
            pe.wait_ge(table_loaded, 16 * 4)
            pe.wait_ge(sel_ready, 1)
            pe.matmul(out_ps[0:GT, 0:EMB], row_sel[:], row_table[:], start=True, stop=True).then_inc(tok_turned, 1)
            pe.wait_ge(wemb_loaded, 32)

            def embed(g):
                if not g.real:
                    return
                if not embedded_from_xpt(g):
                    pe.wait_ge(xs_loaded[g.buf], 16 * xs_turns(g))
                elif g.n == 0:
                    wait_all_x(pe, 0)
                    pe.wait_ge(xpt_zeroed, 1)
                elif g.n == XIMG // GI:
                    wait_all_x(pe, 1)
                if positive(g.n - 1) and emb_bank(g) is emb_ps:
                    pe.wait_ge(qkt_evac, QKT_EVACS * (g.n - 1))
                for f in range(KF):
                    features = xpt[:, f, g.n * GI:(g.n + 1) * GI].rearrange("p b t -> p (b t)") if embedded_from_xpt(g) else xs[:, g.buf, f]
                    mm = pe.matmul(emb_bank(g)[0:GT, 0:EMB], features, wemb[:, f // 2, f % 2], start=(f == 0), stop=(f == KF - 1))
                mm.then_inc(emb_done, 1)

            def turn_xn1(g):
                if not g.real:
                    return
                pe.wait_ge(xn1_done, g.n + 1)
                if emb_bank(g) is not emb_ps and positive(g.n - 1):
                    pe.wait_ge(qkt_evac, QKT_EVACS * (g.n - 1))
                for k in range(KE):
                    mm = pe.transpose(emb_ps[:, k * GT:(k + 1) * GT], xn1[0:GT, g.buf, k * P:(k + 1) * P], ident[0:GT, 0:GT])
                mm.then_inc(x1t_done, 1)

            def project_qk(g):
                if not g.real:
                    return
                pe.wait_ge(x1t_evac, g.n + 1)
                if positive(g.n - 2):
                    pe.wait_ge(pt_evac, 2 * (g.n - 2))
                elif g.n == 2:
                    pe.wait_ge(wt_evac, W_BATCHES)
                for k in range(KE):
                    mm = pe.matmul(ptq_ps0[0:GT], x1t[:, g.buf, k], wqkv[:, k, 0:2 * EMB], start=(k == 0), stop=(k == KE - 1))
                mm.then_inc(qk_done, 1)

            def project_v(g):
                if not g.real:
                    return
                for k in range(KE):
                    mm = pe.matmul(ptq_ps1[0:GT, 0:EMB], x1t[:, g.buf, k], wqkv[:, k, 2 * EMB:QKV], start=(k == 0), stop=(k == KE - 1))
                mm.then_inc(v_done, 1)

            def turn_qk(g):
                if not g.real:
                    return
                pe.wait_ge(qkn_done, g.n + 1)
                if g.real and (not isinstance(g.n, int) or g.n + 1 < NG):
                    pe.wait_ge(x1t_evac, g.n + 2)
                for k in range(2 * KE):
                    mm = pe.transpose(emb_ps[:, k * GT:(k + 1) * GT], qk[0:GT, g.buf, k * P:(k + 1) * P], ident[0:GT, 0:GT])
                mm.then_inc(qkt_done, 1)

            def scores(g):
                if not g.real:
                    return
                pe.wait_ge(qkt_evac, QKT_EVACS * (g.n + 1))
                if positive(g.n):
                    pe.wait_ge(sub_done, g.n)
                else:
                    wait_all_x(pe, 1)
                for a in range(KE):
                    for im in range(GI):
                        bank, at = divmod((im * KE + a) * SIDE_HEADS, BLOCKS // SB)
                        mm = pe.matmul(score_ps[0:GT, bank, at * TOK:(at + SIDE_HEADS) * TOK],
                                       qh[:, a, im].rearrange("p i q -> p (i q)"),
                                       kh[:, a * SIDE_HEADS:(a + 1) * SIDE_HEADS, im * TOK:(im + 1) * TOK], start=True, stop=True)
                mm.then_inc(scores_done, 1)

            def turn_probs(g):
                if not g.real:
                    return
                pe.wait_ge(probs_ready, g.n + 1)
                if not isinstance(g.n, int) or g.n + 2 < NG:
                    pe.wait_ge(qk_ready, g.n + 3)
                    pe.wait_ge(v_ready, g.n + 3)
                for w in range(BLOCKS // 2):
                    im, of_im = divmod(w, SIDE_HEADS)
                    rows = PAIR if of_im == 1 else GT
                    at = im * PT_IM + (0, GT, GT + PAIR)[of_im]
                    b = int(at >= PT_SPLIT)
                    at -= b * PT_SPLIT
                    src = prob[0:rows, g.buf, 2 * w:2 * w + 2].rearrange("p b k -> p (b k)")
                    mm = pe.transpose((ptq_ps0, ptq_ps1)[b][0:PAIR, at:at + rows], src, ident[0:rows, 0:rows])
                    if b == 1 and w == BLOCKS // 2 - 1 or at + rows == PT_SPLIT and b == 0:
                        mm.then_inc(pt_done, 1)

            def attend(g):
                if not g.real:
                    return
                pe.wait_ge(pt_evac, 2 * (g.n + 1))
                pe.wait_ge(v_moved[g.buf], 16 * 2 * GI * (g.turn + 1))
                if positive(g.n):
                    if not isinstance(g.n, int) or x2_bank(Group(0, g.n - 1)) is out_ps:
                        pe.wait_ge(x2lo_done, g.n)
                    else:
                        pe.wait_ge(h2_ready, g.n)
                for a in range(KE):
                    for im in range(GI):
                        for c in range(NPAIR // KE):
                            at = im * PT_IM + (a * (NPAIR // KE) + c) * TOK
                            mm = pe.matmul(out_ps[c * 32:(c + 1) * 32, a * GT + im * TOK:a * GT + (im + 1) * TOK],
                                           v2[:, g.buf, im, :, a * (NPAIR // KE) + c],
                                           pt[:, at:at + TOK], start=True, stop=True)
                mm.then_inc(v2_free, 1)

            def project_out(g):
                if not g.real:
                    return
                pe.wait_ge(ot_evac, g.n + 1)
                for k in range(KE):
                    mm = pe.matmul(out_ps[0:GT, 0:EMB], ot[:, k], wo[:, k], start=(k == 0), stop=(k == KE - 1))
                mm.then_inc(o_done, 1)

            def turn_xn2(g):
                if not g.real:
                    return
                pe.wait_ge(xn2_done, g.n + 1)
                if x2_bank(g) is ptq_ps1:
                    pe.wait_ge(pt_evac, 2 * NG)
                    pe.wait_ge(x2lo_done, g9.n)
                for k in range(KE):
                    mm = pe.transpose(x2_bank(g)[:, k * GT:(k + 1) * GT], xn2[0:GT, k * P:(k + 1) * P], ident[0:GT, 0:GT])
                mm.then_inc(x2t_done, 1)

            def gate_up(c, m):
                if not c.real:
                    return
                T = CG * GT
                if m == 0:
                    pe.wait_ge(x2lo_done, c.n * CG + c.groups)
                n, bank = c.n * MT + m, gu_bank(c, m)
                if not in_tail(c, m):
                    pe.wait_ge(gu_free, n + 1)
                elif tail_tile(c, m) < TAIL_RING:
                    first_use = [(qkt_evac, QKT_EVACS * NG),
                                 (gu_free, n),
                                 (sub_done, NG),
                                 (pt_evac, 2 * NG)]
                    pe.wait_ge(*first_use[tail_tile(c, m)])
                else:
                    pe.wait_ge(gu_free, n + 2 - TAIL_RING)
                for u, w in enumerate((wgt, wut)):
                    for q in range(c.folds):
                        cols, t = T // c.folds, m * c.folds + q
                        for k in range(KE):
                            for part in (x2hi, x2lo):
                                mm = pe.matmul(bank[:, u * T + q * cols:u * T + (q + 1) * cols], w[:, k, t * P:(t + 1) * P],
                                               part[:, k, bass.ds(c.n * T, cols)],
                                               start=(k == 0 and part is x2hi), stop=(k == KE - 1 and part is x2lo))
                mm.then_inc(gu_done, 1)

            def down(c, m):
                if not c.real:
                    return
                pe.wait_ge(hhi_done, c.n * MT + m + 1)
                if m == 0 and acc_bank(c) is acc_ps:
                    pe.wait_ge(acc_free, c.n + 1)
                for part in (hhi, hlo):
                    if part is hlo:
                        pe.wait_ge(hlo_done, c.n * MT + m + 1)
                    for q in range(CG):
                        group, t = (q, m) if c.folds == 1 else (0, m * c.folds + q)
                        mm = pe.matmul(acc_bank(c)[0:GT, group * EMB:(group + 1) * EMB], part[:, ring(c, m), q * GT:(q + 1) * GT], wdt[:, t],
                                       start=(m == 0 and q == 0 and part is hhi), stop=(t == MT - 1 and part is hlo), skip_group_check=True)
                mm.then_inc(down_done, 1)

            def slot(i, s):
                c, first = Chunk(i, s), s % 2 == 1
                if s == 2:
                    turn_ffn_weights(ffn_batches(s)[:-1])
                if s > 0:
                    embed(Group(i, s + 2))
                if s == 1:
                    turn_ffn_weights(ffn_batches(0)[-1:])
                if first:
                    down(Chunk(i, s - 2), 5)
                if not first:
                    down(c, 1)
                    gate_up(c, 3)
                    down(c, 2)
                if s > FFN_SLOT:
                    turn_xn2(Group(i, s - 2))
                turn_probs(Group(i, s - 1))
                if s <= FFN_SLOT:
                    turn_xn2(Group(i, s - 2))
                scores(Group(i, s))
                if s == 0:
                    project_qk(g2)
                    project_v(g2)
                if 0 <= s < 2:
                    turn_ffn_weights(ffn_batches(s)[:-1])
                gate_up(c, 0 if first else 4)
                if s == FFN_SLOT:
                    attend(Group(i, s - 1))
                if s > 0:
                    turn_xn1(Group(i, s + 2))
                if not first:
                    down(c, 3)
                if s != FFN_SLOT:
                    attend(Group(i, s - 1))
                if 1 <= s < 3:
                    turn_ffn_weights(ffn_batches(s)[-1:])
                if not first:
                    turn_qk(Group(i, s + 1))
                if s > 0:
                    project_qk(Group(i, s + 2))
                if first:
                    turn_qk(Group(i, s + 1))
                gate_up(c, 1 if first else 5)
                if s > 0:
                    project_v(Group(i, s + 2))
                down(c, 0 if first else 4)
                project_out(Group(i, s - 1))
                if first:
                    gate_up(c, 2)

            def turn_ffn_weights(batches):
                pe.wait_ge(ident16_ready, 1)
                pe.wait_ge(w16_ready, batches[0] * FW_BATCH // FW_SETS + 1)
                for b in batches:
                    if b == 0:
                        wait_all_x(pe, 1)
                    if b >= 2:
                        pe.wait_ge(fwt_evac, b - 1)
                    for q in range(FW_BATCH):
                        w, n = divmod(b * FW_BATCH + q, FW_SETS)
                        src = w16[:, w, n * P:(n + 1) * P]
                        mm = pe.transpose(spare_ps[:, b % 2].bitcast(F16)[:, q * P:(q + 1) * P], src, ident16[:])
                    mm.then_inc(fwt_done, 1)

            embed(g0)
            pe.wait_ge(tok_added, 1)
            embed(g1)
            turn_xn1(g0)
            pe.wait_ge(wt_evac, 4)
            pe.wait_ge(qkv_w_centred, KE)
            project_qk(g0)
            project_v(g0)
            turn_xn1(g1)
            embed(g2)
            pe.wait_ge(qk_ready, 1)
            pe.wait_ge(v_ready, 1)
            project_qk(g1)
            project_v(g1)
            turn_x(1, range(XCUT_FIRST))
            turn_qk(g0)
            turn_x(1, range(XCUT_FIRST, KF))
            pe.wait_ge(wo_ordered, KE * PIECES)
            pe.wait_ge(qk_ready, 2)
            pe.wait_ge(v_ready, 2)
            turn_weights(wo_pairs, KE, KE, 4)
            turn_xn1(g2)
            slots(pe, slot)
            turn_probs(g8)
            scores(g9)
            down(c2, 5)
            attend(g8)
            turn_xn2(g7)
            project_out(g8)
            gate_up(c3, 0)
            turn_qk(g10)
            gate_up(c3, 1)
            down(c3, 0)
            gate_up(c3, 2)

            scores(g10)
            down(c3, 1)
            gate_up(c3, 3)
            turn_probs(g9)
            turn_xn2(g8)
            down(c3, 2)
            gate_up(c3, 4)
            attend(g9)
            down(c3, 3)
            project_out(g9)
            gate_up(c3, 5)

            turn_probs(g10)
            down(c3, 4)
            attend(g10)
            turn_xn2(g9)
            down(c3, 5)
            project_out(g10)
            gate_up(c4, 0)
            gate_up(c4, 1)
            gate_up(c4, 2)
            gate_up(c4, 3)
            turn_xn2(g10)
            down(c4, 0)
            gate_up(c4, 4)
            down(c4, 1)
            gate_up(c4, 5)
            for m in range(c5.tiles):
                down(c4, m + 2)
                gate_up(c5, m)
            down(c4, 5)
            for m in range(c5.tiles):
                down(c5, m)

        @block.scalar
        def _(act):
            def evac_x(batches):
                for n in (b for b in batches if not dve_evacuates(b)):
                    act.wait_ge(xt_done, n + 1)
                    nc.scalar.copy(x_patches(n), x_turned(n)).then_inc(xt_evac_act, 1)

            def cut_x(t, features):
                for f in features:
                    act.wait_ge(x_loaded[t][f // 2], 16)
                    act.wait_ge(xt_done, XT_BATCHES * (t - 1) + 2 * (f + 1))
                    nc.scalar.copy(xcut_at(f), half_patches(t, f)).then_inc(xcut_ready[t], 1)

            def load_xs(g):
                if embedded_from_xpt(g):
                    return
                if isinstance(g.n, int) and g.n == FIRST_XS:
                    for load in range(XTILES):
                        wait_all_x(act, load)
                    act.wait_ge(xpt_zeroed, 1)
                act.wait_ge(emb_done, g.n - 1)
                act.dma_start(xs[:, g.buf], xpt.rearrange("p k b t -> p k (b t)")[:, :, bass.ds(g.n * GT, GT)]).then_inc(xs_loaded[g.buf], 16)

            for m in range(4):
                act.wait_ge(wt_done, m + 1)
                src = (ptq_ps0, ptq_ps1)[m % 2]
                if m % 2 == 0:
                    cp = nc.scalar.copy(wqkv[:, m // 2, 0:3 * P], src[:, 0:3 * P])
                else:
                    nc.scalar.copy(wqkv[:, m // 2, 3 * P:4 * P], src[:, 0:P])
                    for to, of in pair_order(wqkv[:, m // 2, 2 * EMB:QKV], src[:, P:3 * P]):
                        cp = nc.scalar.copy(to, of)
                cp.then_inc(wt_evac, 1)
            evac_x(range(2))
            act.wait_ge(x_loaded[0][CH - 1], 16)
            nc.scalar.copy(xcut_at(KF - 1), half_patches(0, KF - 1)).then_inc(xcut_last_ready, 1)
            evac_x(range(2, XT_BATCHES))

            def evac_pt(g):
                if not g.real:
                    return
                if positive(g.n):
                    act.wait_ge(v2_free, g.n + 2)
                for b in range(2):
                    act.wait_ge(pt_done, 2 * g.n + b + 1)
                    cols = slice(PT_SPLIT) if b == 0 else slice(PT_SPLIT, GI * PT_IM)
                    nc.scalar.copy(pt[:, cols], (ptq_ps0, ptq_ps1)[b][0:PAIR, 0:(PT_SPLIT, GI * PT_IM - PT_SPLIT)[b]]).then_inc(pt_evac, 1)

            def exponentials(g):
                if not g.real:
                    return
                act.wait_ge(sub_done, g.n + 1)
                view = prob[0:GT, g.buf].rearrange("p b k -> p (b k)")
                nc.scalar.activation(view, view, ACT.Exp, scale=float(HD) ** -0.5).then_inc(exp_done, 1)

            def evac_ot(g):
                if not g.real:
                    return
                if positive(g.n):
                    act.wait_ge(o_done, g.n)
                act.wait_ge(v2_free, g.n + 3)
                nc.scalar.copy(ot[:], out_ps[:, 0:KE * GT].rearrange("p (k t) -> p k t", k=KE)).then_inc(ot_evac, 1)

            def evac_x1t(g):
                if not g.real:
                    return
                act.wait_ge(x1t_done, g.n + 1)
                nc.scalar.copy(x1t[:, g.buf], emb_ps[:, 0:KE * GT].rearrange("p (k t) -> p k t", k=KE)).then_inc(x1t_evac, 1)

            def evac_kt(g, copies):
                if not g.real:
                    return
                for c in copies:
                    act.wait_ge(qkt_done, g.n + 1)
                    nc.scalar.activation(kh[:, kh_slots(c)], emb_ps[:, KE * GT:2 * KE * GT].rearrange("p (a t) -> p a t", a=KE),
                                         ACT.Identity, bias=kln[:, 2, c:c + 1], scale=kln[:, 1, c:c + 1]).then_inc(qkt_evac, 1)

            def evac_qt(g, copies):
                if not g.real:
                    return
                for c in copies:
                    act.wait_ge(qkt_done, g.n + 1)
                    nc.scalar.activation(qh[:, :, :, c], emb_ps[:, 0:KE * GT].rearrange("p (a i t) -> p a i t", a=KE, i=GI),
                                         ACT.Identity, bias=qln[:, 2, c:c + 1], scale=qln[:, 1, c:c + 1]).then_inc(qkt_evac, 1)

            def squares(g):
                if not g.real:
                    return
                act.wait_ge(qk_ready, g.n + 1)
                if positive(g.n):
                    act.wait_ge(ss_done, g.n)
                nc.scalar.activation(sq[0:GT], qk[0:GT, g.buf], ACT.Square).then_inc(sq_done, 1)

            def high_x2(g):
                if not g.real:
                    return
                act.wait_ge(x2t_done, g.n + 1)
                nc.scalar.copy(x2hi[:, :, bass.ds(g.n * GT, GT)], x2_bank(g)[:, 0:KE * GT].rearrange("p (k t) -> p k t", k=KE)).then_inc(x2hi_done, 1)

            def tanh_gate(c, m):
                if not c.real:
                    return
                T = CG * GT
                act.wait_ge(gu_done, c.n * MT + m + 1)
                nc.scalar.activation(th[:, ring(c, m), 0:T], gu_bank(c, m)[:, 0:T], ACT.Tanh, scale=0.5 * QUANT / XSCALE).then_inc(tanh_done, 1)

            def high_hidden(c, m):
                if not c.real:
                    return
                T = CG * GT
                act.wait_ge(gu_free, c.n * MT + m + 2)
                nc.scalar.copy(hhi[:, ring(c, m), 0:T], hf[:, ring(c, m), 0:T]).then_inc(hhi_done, 1)

            def slot(i, s):
                c, first = Chunk(i, s), s % 2 == 1
                load_xs(Group(i, s + 3))
                if not first:
                    tanh_gate(c, 3)
                high_x2(Group(i, s - 2))
                evac_pt(Group(i, s - 1))
                if not first:
                    high_hidden(c, 3)
                if s == 0:
                    exponentials(g0)
                if 0 <= s < 3:
                    evac_ffn_weights(ffn_batches(s)[:-1])
                if s > 0:
                    evac_x1t(Group(i, s + 2))
                if s < FFN_SLOT:
                    evac_ot(Group(i, s - 1))
                    if s > 0:
                        evac_ffn_weights(ffn_batches(s)[-1:])
                        exponentials(Group(i, s))
                    evac_kt(Group(i, s + 1), range(SIDE_HEADS))
                    if s == 0:
                        squares(g2)
                    evac_qt(Group(i, s + 1), range(SIDE_HEADS))
                    if s == 0:
                        evac_ffn_weights(ffn_batches(s)[-1:])
                else:
                    tanh_gate(c, 0 if first else 4)
                    exponentials(Group(i, s))
                    high_hidden(c, 0 if first else 4)
                    evac_ot(Group(i, s - 1))
                    evac_kt(Group(i, s + 1), range(SIDE_HEADS))
                    tanh_gate(c, 1 if first else 5)
                    evac_qt(Group(i, s + 1), range(SIDE_HEADS))
                if s > 0:
                    squares(Group(i, s + 2))
                high_hidden(c, 1 if first else 5)
                if first:
                    tanh_gate(c, 2)
                    high_hidden(c, 2)

            def evac_ffn_weights(batches):
                last = 3 * FW_SETS // FW_BATCH - 1
                for b in batches:
                    done = {last - 1: acc_free, last: gu_free}.get(b, fwt_evac)
                    act.wait_ge(fwt_done, b + 1)
                    w, n = divmod(b * FW_BATCH, FW_SETS)
                    src = spare_ps[:, b % 2].bitcast(F16)[:, 0:FW_BATCH * P]
                    if w < 2:
                        dst = (wgt, wut)[w].rearrange("p k (m c) -> p m k c", c=P)[:, n // KE:(n + FW_BATCH) // KE]
                        nc.scalar.copy(dst, src.rearrange("p (m k c) -> p m k c", k=KE, c=P)).then_inc(done, 1)
                    else:
                        for q in range(FW_BATCH):
                            k, m = divmod(n + q, MT)
                            cp = nc.scalar.copy(wdt[:, m, k * P:(k + 1) * P], src[:, q * P:(q + 1) * P])
                        cp.then_inc(done, 1)

            cut_x(1, range(ACT_CUTS // 2))
            evac_x1t(g0)
            evac_x1t(g1)
            squares(g0)
            cut_x(1, range(ACT_CUTS // 2, ACT_CUTS))
            evac_x(range(XT_BATCHES, XT_BATCHES + 2 * XCUT_FIRST))
            act.wait_ge(qln_ready, 4)
            evac_kt(g0, range(SIDE_HEADS))
            evac_qt(g0, range(SIDE_HEADS))
            evac_x(range(XT_BATCHES + 2 * XCUT_FIRST, 2 * XT_BATCHES))
            for m in range(4, 6):
                act.wait_ge(wt_done, m + 1)
                nc.scalar.copy(wo[:, m - 4], (ptq_ps0, ptq_ps1)[m % 2][:, 0:EMB]).then_inc(wt_evac, 1)
            evac_x1t(g2)
            slots(act, slot)
            evac_pt(g8)
            evac_ot(g8)
            high_x2(g7)
            tanh_gate(c3, 0)
            evac_kt(g10, range(1))
            high_hidden(c3, 0)
            evac_kt(g10, range(1, 2))
            tanh_gate(c3, 1)
            exponentials(g9)
            evac_kt(g10, range(2, SIDE_HEADS))
            evac_qt(g10, range(SIDE_HEADS))
            high_hidden(c3, 1)
            tanh_gate(c3, 2)
            high_hidden(c3, 2)
            tanh_gate(c3, 3)
            evac_pt(g9)
            high_x2(g8)
            high_hidden(c3, 3)
            exponentials(g10)
            tanh_gate(c3, 4)
            evac_ot(g9)
            high_hidden(c3, 4)
            tanh_gate(c3, 5)
            evac_pt(g10)
            high_hidden(c3, 5)
            evac_ot(g10)
            high_x2(g9)
            tiles = [(c4, m) for m in range(MT)] + [(c5, m) for m in range(c5.tiles)]
            tanh_gate(*tiles[0])
            for n, tile in enumerate(tiles):
                if n + 1 < len(tiles):
                    tanh_gate(*tiles[n + 1])
                if n == 2:
                    high_x2(g10)
                high_hidden(*tile)
            act.wait_ge(xs_loaded[NG % 2], 16 * xs_turns(Group(0, NG)))

        @block.vector
        def _(dve):
            dve.wait_ge(ident_ready, 1)
            nc.vector.tensor_copy(ident16[:], ident[:]).then_inc(ident16_ready, 1)
            nc.vector.memset(par[:], 0.0).then_inc(par_ready, 1)
            dve.wait_ge(par_ready, 1)
            nc.vector.tensor_reduce(par[:, 0:CH_HEADS], ident.rearrange("p (r d) -> p r d", d=HD), AX.X, ALU.add).then_inc(par_ready, 1)
            dve.wait_ge(par_ready, 2)
            nc.vector.tensor_reduce(qln[:, 0], par.rearrange("p (i j) -> p i j", j=SIDE_HEADS), AX.X, ALU.add).then_inc(par_ready, 1)
            nc.vector.tensor_reduce(kln[:, 0], par.rearrange("p (i j) -> p j i", j=SIDE_HEADS), AX.X, ALU.add).then_inc(par_ready, 1)

            for f in range(KF - 1):
                dve.wait_ge(x_loaded[0][f // 2], 16)
                nc.vector.tensor_copy(xcut_at(f), half_patches(0, f)).then_inc(xcut_ready[0], 1)
            def evac_x(batches):
                for n in (b for b in batches if dve_evacuates(b)):
                    dve.wait_ge(xt_done, n + 1)
                    nc.vector.tensor_copy(x_patches(n), x_turned(n)).then_inc(xt_evac_dve, 1)

            evac_x(range(XT_BATCHES))
            dve.wait_ge(tok_turned, 1)
            nc.vector.tensor_copy(tok_add[0:GT], out_ps[0:GT, 0:EMB]).then_inc(tok_added, 1)
            dve.wait_ge(wt_evac, 4)
            for k in range(KE):
                nc.vector.tensor_reduce(wmean[:, k], wqkv[:, k, 0:2 * EMB].rearrange("p (h d) -> p h d", d=HD), AX.X, ALU.add).then_inc(means_done, 1)
            for k in range(KE):
                dve.wait_ge(means_done, KE + k)
                nc.vector.tensor_scalar(wmean[:, k], wmean[:, k], 1.0 / HD, None, ALU.mult).then_inc(means_done, 1)
                dve.wait_ge(means_done, KE + k + 1)
                view = wqkv[:, k, 0:2 * EMB].rearrange("p (h d) -> p h d", d=HD)
                nc.vector.tensor_tensor(view, view, wmean[:, k].unsqueeze(2).to_broadcast([P, 2 * HEADS, HD]), ALU.subtract).then_inc(qkv_w_centred, 1)
            dve.wait_ge(tok_added, 1)

            bview = bqkv[0:GT, 0:2 * EMB].rearrange("p (h d) -> p h d", d=HD)

            def sum_bias():
                dve.wait_ge(rows_loaded, 16 * 2)
                nc.vector.tensor_reduce(bmean[0:GT], bview, AX.X, ALU.add).then_inc(bmeans_done, 1)

            def centre_bias():
                dve.wait_ge(bmeans_done, 1)
                nc.vector.tensor_scalar(bmean[0:GT], bmean[0:GT], 1.0 / HD, None, ALU.mult).then_inc(bmeans_done, 1)
                dve.wait_ge(bmeans_done, 2)
                nc.vector.tensor_tensor(bview, bview, bmean[0:GT].unsqueeze(2).to_broadcast([GT, 2 * HEADS, HD]), ALU.subtract).then_inc(qkv_w_centred, 1)
                dve.wait_ge(qkv_w_centred, KE + 1)

            def pair_v_bias():
                for to, of in pair_order(bv[0:GT], bqkv[0:GT, 2 * EMB:QKV]):
                    nc.vector.tensor_copy(to, of).then_inc(bv_ready, 1)
                dve.wait_ge(bv_ready, PIECES)

            def place_ln_params():
                dve.wait_ge(cols_loaded, 16 * 4)
                dve.wait_ge(par_ready, 4)
                for side, ln in enumerate((qln, kln)):
                    for n in range(2):
                        nc.vector.tensor_scalar(ln[:, 1 + n], ln[:, 0], lnp[:, 2 * side + n:2 * side + n + 1], None, ALU.mult).then_inc(qln_ready, 1)

            def score_view():
                return score_ps[0:GT, :, 0:BLOCKS // SB * TOK].rearrange("p j (b k) -> p j b k", k=TOK)

            def score_maximum(g):
                if not g.real:
                    return
                dve.wait_ge(scores_done, g.n + 1)
                nc.vector.tensor_reduce(smax[0:GT, g.buf].rearrange("p (j b) -> p j b", j=SB), score_view(), AX.X, ALU.max).then_inc(max_done, 1)

            def shift_scores(g):
                if not g.real:
                    return
                dve.wait_ge(max_done, g.n + 1)
                if positive(g.n - 1):
                    dve.wait_ge(pt_done, 2 * (g.n - 1))
                nc.vector.tensor_tensor(prob[0:GT, g.buf].rearrange("p (j b) k -> p j b k", j=SB), score_view(),
                                        smax[0:GT, g.buf].rearrange("p (j b) -> p j b", j=SB).unsqueeze(3).to_broadcast([GT, SB, BLOCKS // SB, TOK]),
                                        ALU.subtract).then_inc(sub_done, 1)

            def cast_ffn_weight(w):
                dve.wait_ge(ffn_loaded[w], 16)
                nc.vector.tensor_copy(w16[:, w], wraw[:, w]).then_inc(w16_ready, 1)

            def embed_tokens(g):
                if not g.real:
                    return
                dve.wait_ge(emb_done, g.n + 1)
                if positive(g.n - 1):
                    dve.wait_ge(res_ready, g.n - 1)
                nc.vector.tensor_tensor(h_emb[0:GT, g.buf], emb_bank(g)[0:GT, 0:EMB], tok_add[0:GT], ALU.add).then_inc(h_ready, 1)
                dve.wait_ge(h_ready, g.n + 1)
                nc.vector.bn_stats(stats1[0:GT, g.buf], h_emb[0:GT, g.buf]).then_inc(stats1_done, 1)

            def token_variance(g):
                if not g.real:
                    return
                nc.vector.bn_aggr(mv1[0:GT, g.buf], stats1[0:GT, g.buf]).then_inc(mv1_done, 1)
                dve.wait_ge(mv1_done, g.n + 1)
                nc.vector.tensor_scalar(ve1[0:GT, g.buf:g.buf + 1], mv1[0:GT, g.buf, 1:2], LN_EPS, None, ALU.add).then_inc(ve1_done, 1)

            def sum_probs(g):
                if not g.real:
                    return
                dve.wait_ge(exp_done, g.n + 1)
                nc.vector.tensor_reduce(ssum[0:GT, g.buf], prob[0:GT, g.buf], AX.X, ALU.add).then_inc(sum_done, 1)
                dve.wait_ge(sum_done, g.n + 1)
                nc.vector.reciprocal(rsum[0:GT, g.buf], ssum[0:GT, g.buf]).then_inc(rsum_done, 1)

            def norm_tokens(g):
                if not g.real:
                    return
                dve.wait_ge(rstd1_done, g.n + 1)
                if positive(g.n - 1):
                    dve.wait_ge(x1t_done, g.n - 1)
                nc.vector.tensor_scalar(xn1[0:GT, g.buf], h_emb[0:GT, g.buf], mv1[0:GT, g.buf, 0:1], rstd1[0:GT, g.buf:g.buf + 1],
                                        ALU.subtract, ALU.mult).then_inc(xn1_done, 1)

            def add_attention(g):
                if not g.real:
                    return
                dve.wait_ge(o_done, g.n + 1)
                dve.wait_ge(res_ready, g.n + 1)
                if positive(g.n):
                    dve.wait_ge(h2_kept, g.n)
                nc.vector.tensor_tensor(hcur[0:GT], out_ps[0:GT, 0:EMB], h2[0:GT, g.n], ALU.add).then_inc(h2_ready, 1)
                dve.wait_ge(h2_ready, g.n + 1)
                nc.vector.bn_stats(stats2[0:GT], hcur[0:GT]).then_inc(stats2_done, 1)

            def residual_variance(g):
                if not g.real:
                    return
                nc.vector.bn_aggr(mv2[0:GT], stats2[0:GT]).then_inc(mv2_done, 1)
                dve.wait_ge(mv2_done, g.n + 1)
                nc.vector.tensor_scalar(ve2[0:GT], mv2[0:GT, 1:2], LN_EPS, XSCALE ** -2, ALU.add, ALU.mult).then_inc(ve2_done, 1)

            def norm_residual(g):
                if not g.real:
                    return
                dve.wait_ge(rstd2_done, g.n + 1)
                nc.vector.tensor_scalar(xn2[0:GT], hcur[0:GT], mv2[0:GT, 0:1], rstd2[0:GT], ALU.subtract, ALU.mult).then_inc(xn2_done, 1)

            def bias_qk(g):
                if not g.real:
                    return
                dve.wait_ge(qk_done, g.n + 1)
                if positive(g.n - 1):
                    dve.wait_ge(qkt_done, g.n - 1)
                nc.vector.tensor_tensor(qk[0:GT, g.buf], ptq_ps0[0:GT], bqkv[0:GT, 0:2 * EMB], ALU.add).then_inc(qk_ready, 1)

            def bias_v(g):
                if not g.real:
                    return
                dve.wait_ge(v_done, g.n + 1)
                if positive(g.turn):
                    dve.wait_ge(v_moved[g.buf], 16 * 2 * GI * g.turn)
                nc.vector.tensor_tensor(vt[0:GT, g.buf].rearrange("p q d c -> p q c d"), ptq_ps1[0:GT, 0:EMB].rearrange("p (c q d) -> p q c d", q=2, d=HD),
                                        bv[0:GT].rearrange("p (c q d) -> p q c d", q=2, d=HD), ALU.add).then_inc(v_ready, 1)

            def sum_squares(g):
                if not g.real:
                    return
                dve.wait_ge(sq_done, g.n + 1)
                nc.vector.tensor_reduce(ss[0:GT, g.buf], sq[0:GT].rearrange("p (h d) -> p h d", d=HD), AX.X, ALU.add).then_inc(ss_done, 1)

            def variance_qk(g):
                if not g.real:
                    return
                dve.wait_ge(ss_done, g.n + 1)
                nc.vector.tensor_scalar(ve_qk[0:GT], ss[0:GT, g.buf], 1.0 / HD, LN_EPS, ALU.mult, ALU.add).then_inc(ve_qk_done, 1)

            def guess_rstd(g):
                if not g.real:
                    return
                y, half = rstd_qk[0:GT, g.buf], newton[0:GT]
                dve.wait_ge(ve_qk_done, g.n + 1)
                if positive(g.n - 1):
                    dve.wait_ge(qkn_done, g.n - 1)
                nc.vector.tensor_scalar(half.bitcast(I32), ve_qk[0:GT].bitcast(I32), 1, None, ALU.arith_shift_right).then_inc(newton_done, 1)
                dve.wait_ge(newton_done, g.n * NEWTON_OPS + 1)
                nc.vector.tensor_scalar(y.bitcast(I32), half.bitcast(I32), -1.0, RSQRT_MAGIC, ALU.mult, ALU.add).then_inc(newton_done, 1)

            def newton_turn(g, t):
                if not g.real:
                    return
                y, half = rstd_qk[0:GT, g.buf], newton[0:GT]
                count = g.n * NEWTON_OPS + 3 * t + 2
                dve.wait_ge(newton_done, count)
                nc.vector.scalar_tensor_tensor(out=half, in0=y, scalar=-0.5, in1=y, op0=ALU.mult, op1=ALU.mult).then_inc(newton_done, 1)
                dve.wait_ge(newton_done, count + 1)
                nc.vector.tensor_tensor(half, half, ve_qk[0:GT], ALU.mult).then_inc(newton_done, 1)
                dve.wait_ge(newton_done, count + 2)
                nc.vector.scalar_tensor_tensor(out=y, in0=half, scalar=1.5, in1=y, op0=ALU.add, op1=ALU.mult)\
                    .then_inc(newton_done if t < NEWTON_TURNS - 1 else rstd_qk_done, 1)

            def low_x2(g):
                if not g.real:
                    return
                dve.wait_ge(x2hi_done, g.n + 1)
                nc.vector.tensor_tensor(x2lo[:, :, bass.ds(g.n * GT, GT)], x2_bank(g)[:, 0:KE * GT].rearrange("p (k t) -> p k t", k=KE),
                                        x2hi[:, :, bass.ds(g.n * GT, GT)], ALU.subtract).then_inc(x2lo_done, 1)

            def hidden(c, m):
                if not c.real:
                    return
                n, T = c.n * MT + m, CG * GT
                dve.wait_ge(tanh_done, n + 1)
                nc.vector.scalar_tensor_tensor(out=th[:, ring(c, m), 0:T], in0=th[:, ring(c, m), 0:T], scalar=1.0, in1=gu_bank(c, m)[:, 0:T],
                                               op0=ALU.add, op1=ALU.mult).then_inc(gated_done, 1)
                dve.wait_ge(gated_done, n + 1)
                nc.vector.scalar_tensor_tensor(out=hf[:, ring(c, m), 0:T], in0=gu_bank(c, m)[:, T:2 * T], scalar=0.5 * (QUANT / XSCALE) ** 2 * HSCALE,
                                               in1=th[:, ring(c, m), 0:T], op0=ALU.mult, op1=ALU.mult).then_inc(gu_free, 1)

            def add_ffn(c):
                if not c.real:
                    return
                dve.wait_ge(down_done, c.n * MT + c.tiles)
                dve.wait_ge(h2_kept, c.n * CG + c.groups)
                for q in range(c.groups):
                    row = h2[0:GT, c.n * CG + q]
                    y = nc.vector.scalar_tensor_tensor(out=row, in0=acc_bank(c)[0:GT, q * EMB:(q + 1) * EMB], scalar=QUANT / HSCALE,
                                                       in1=row, op0=ALU.mult, op1=ALU.add)
                y.then_inc(acc_free, 1)

            def slot(i, s):
                embedded, attended = Group(i, s + 2), Group(i, s - 1)
                c, first = Chunk(i, s), s % 2 == 1
                if s > 0:
                    if s > 1:
                        embed_tokens(embedded)
                    if first:
                        low_x2(Group(i, s - 2))
                    if s > 1 and embedded.real:
                        dve.wait_ge(stats1_done, embedded.n + 1)
                    newton_turn(Group(i, s + 1), 0)
                    if s > 1:
                        token_variance(embedded)
                    newton_turn(Group(i, s + 1), 1)
                    if s > 1:
                        norm_tokens(embedded)
                    if not first:
                        hidden(c, 3)
                        low_x2(Group(i, s - 2))
                    newton_turn(Group(i, s + 1), 2)
                score_maximum(Group(i, s))
                shift_scores(Group(i, s))
                if 0 <= s < 2:
                    cast_ffn_weight(s + 1)
                hidden(c, 0 if first else 4)
                if first:
                    add_ffn(Chunk(i, s - 2))
                sum_probs(Group(i, s))
                bias_qk(embedded)
                hidden(c, 1 if first else 5)
                bias_v(embedded)
                if s == 0:
                    embed_tokens(g3)
                    dve.wait_ge(stats1_done, g3.n + 1)
                    token_variance(g3)
                add_attention(attended)
                if attended.real:
                    dve.wait_ge(stats2_done, attended.n + 1)
                sum_squares(embedded)
                residual_variance(attended)
                if first:
                    hidden(c, 2)
                variance_qk(embedded)
                guess_rstd(embedded)
                if s == 0:
                    norm_tokens(g3)
                norm_residual(attended)

            for g, while_rstd in ((g0, sum_bias), (g1, centre_bias)):
                embed_tokens(g)
                dve.wait_ge(stats1_done, g.n + 1)
                token_variance(g)
                while_rstd()
                norm_tokens(g)
            bias_qk(g0)
            pair_v_bias()
            bias_v(g0)
            sum_squares(g0)
            variance_qk(g0)
            guess_rstd(g0)
            for t in range(NEWTON_TURNS):
                newton_turn(g0, t)
            bias_qk(g1)
            bias_v(g1)
            place_ln_params()
            embed_tokens(g2)
            dve.wait_ge(stats1_done, g2.n + 1)
            token_variance(g2)
            evac_x(range(XT_BATCHES, XTILES * XT_BATCHES))
            norm_tokens(g2)
            sum_squares(g1)
            variance_qk(g1)
            guess_rstd(g1)
            for t in range(NEWTON_TURNS):
                newton_turn(g1, t)
            cast_ffn_weight(0)
            slots(dve, slot)
            newton_turn(g10, 0)
            newton_turn(g10, 1)
            low_x2(g7)
            newton_turn(g10, 2)
            score_maximum(g9)
            hidden(c3, 0)
            shift_scores(g9)
            add_ffn(c2)
            hidden(c3, 1)
            add_attention(g8)
            sum_probs(g9)
            dve.wait_ge(stats2_done, g8.n + 1)
            residual_variance(g8)
            hidden(c3, 2)
            score_maximum(g10)
            shift_scores(g10)
            norm_residual(g8)
            hidden(c3, 3)
            low_x2(g8)
            sum_probs(g10)
            hidden(c3, 4)
            add_attention(g9)
            dve.wait_ge(stats2_done, g9.n + 1)
            residual_variance(g9)
            hidden(c3, 5)
            norm_residual(g9)
            low_x2(g9)
            add_ffn(c3)
            add_attention(g10)
            dve.wait_ge(stats2_done, g10.n + 1)
            residual_variance(g10)
            hidden(c4, 0)
            norm_residual(g10)
            hidden(c4, 1)
            hidden(c4, 2)
            low_x2(g10)
            hidden(c4, 3)
            hidden(c4, 4)
            hidden(c4, 5)
            hidden(c5, 0)
            hidden(c5, 1)
            hidden(c5, 2)
            add_ffn(c4)
            add_ffn(c5)


_INS = ["x", "cls_tok", "L0_tok_W", "L0_tok_b", "L0_tok_cls_token", "L0_tok_pos_emb", "L0_attn_qkv_w", "L0_attn_qkv_b",
        "L0_attn_o_w", "L0_attn_o_b", "L0_attn_q_norm_w", "L0_attn_q_norm_b", "L0_attn_k_norm_w", "L0_attn_k_norm_b",
        "L0_ffn_w_gate", "L0_ffn_w_up", "L0_ffn_w_down"]


def kernel(**inputs):
    import numpy as _np
    import concourse.bacc as _bacc
    from concourse.bass_utils import run_bass_kernel_spmd as _run

    nc = _bacc.Bacc("TRN2", target_bir_lowering=False, num_devices=1)
    arrays, args = {}, []
    for name in _INS:
        a = _np.ascontiguousarray(inputs[name])
        arrays[f"in_{name}"] = a
        args.append(nc.dram_tensor(f"in_{name}", a.shape, mybir.dt.from_np(a.dtype), kind="ExternalInput").ap())
    args.append(nc.dram_tensor("out_0", (IMAGES, TOK, EMB), F32, kind="ExternalOutput").ap())
    vit_kernel(nc, *args)
    r = _run(nc, [arrays], core_ids=[0])
    return r.results[0]["out_0"]
```
